# Optimizing a Trainium2 kernel written in Bass

```python
import numpy as np
import jax
import jax.numpy as jnp

def _softmax(x, axis=-1):
    return jax.nn.softmax(x, axis=axis)

def _gelu(x):
    return jax.nn.gelu(x, approximate=True)

def _silu(x):
    return jax.nn.silu(x)

def _sigmoid(x):
    return jax.nn.sigmoid(x)

def _layernorm(x, axis=-1, eps=1e-05):
    m = jnp.mean(x, axis=axis, keepdims=True)
    v = jnp.var(x, axis=axis, keepdims=True)
    return (x - m) / jnp.sqrt(v + eps)

def _scatter_add(tgt, idx, src, axis=0):
    return tgt.at[idx].add(src)

def _segment_sum(src, seg, n):
    return jax.ops.segment_sum(src, seg, n)
kernel_name = 'mk_lm_tower_d1_tok_ids4096_r4_5703ee'

def setup_inputs(seed: int=0):
    np.random.seed(seed)
    _w = jnp.asarray

    def _rec_inputs():
        import jax
        import jax.numpy as jnp
        _rk = jax.random.key(seed)
        x = jax.random.randint(jax.random.fold_in(_rk, 1), (4, 512), 0, 50399, jnp.int32)
        return x
    x = _rec_inputs()

    def _L0_tok_setup():
        import jax, jax.numpy as jnp
        import numpy as np
        SHARDS = 8
        VOCAB = 12600
        VS = VOCAB // SHARDS
        D = 1024
        SEQ = 512
        B = 4
        key = jax.random.key(seed)
        k1, k2, k3 = jax.random.split(key, 3)
        x = jax.random.randint(k1, (B, SEQ), 0, VOCAB, dtype=jnp.int32)
        kernel = jax.random.normal(k2, (SHARDS, VS, D), jnp.float32) * (1.0 / np.sqrt(VOCAB))
        bias = jnp.zeros((D,), jnp.float32)
        pos_emb = jax.random.normal(k3, (SEQ, D), jnp.float32) * 0.02
        return {'x': x, 'kernel': kernel, 'bias': bias, 'pos_emb': pos_emb}
    _L0_tok_all = _L0_tok_setup()
    _L0_tok_in = {k: v for k, v in _L0_tok_all.items() if k in ('kernel', 'bias', 'pos_emb')}
    del _L0_tok_all

    def _L0_attn_setup():
        import jax, jax.numpy as jnp
        import numpy as np
        B, S, EMB = (2, 512, 1024)
        NHEADS, KVHEADS, HEAD_D = (32, 8, 128)
        SPLITS = (NHEADS * HEAD_D, KVHEADS * HEAD_D, KVHEADS * HEAD_D)
        key = jax.random.key(seed)
        k1, k2, k3 = jax.random.split(key, 3)
        q = jax.random.normal(k1, (B, S, EMB), dtype=jnp.float32)
        w_qkv = jax.random.normal(k2, (sum(SPLITS), EMB), dtype=jnp.float32) * 0.02
        w_dense = jax.random.normal(k3, (EMB, NHEADS * HEAD_D), dtype=jnp.float32) * 0.02
        return {'q': q, 'w_qkv': w_qkv, 'w_dense': w_dense}
    _L0_attn_all = _L0_attn_setup()
    _L0_attn_in = {k: v for k, v in _L0_attn_all.items() if k in ('w_qkv', 'w_dense')}
    del _L0_attn_all

    def _L0_ffn_setup():
        import jax, jax.numpy as jnp
        import numpy as np
        B, L, H, Dh, M = (4, 512, 16, 64, 256)
        D = H * Dh
        key = jax.random.key(seed)
        kx, ku, kd, kp = jax.random.split(key, 4)
        x = jax.random.normal(kx, (B, L, D), dtype=jnp.float32)
        up = jax.random.normal(ku, (H, Dh, M), dtype=jnp.float32)
        down = jax.random.normal(kd, (H, M, Dh), dtype=jnp.float32)
        perm = jax.random.permutation(kp, D)
        return {'x': x, 'up': up, 'down': down, 'perm': perm}
    _L0_ffn_all = _L0_ffn_setup()
    _L0_ffn_in = {k: v for k, v in _L0_ffn_all.items() if k in ('up', 'down', 'perm')}
    del _L0_ffn_all
    return {'x': x, 'L0_tok_kernel': _L0_tok_in['kernel'], 'L0_tok_bias': _L0_tok_in['bias'], 'L0_tok_pos_emb': _L0_tok_in['pos_emb'], 'L0_attn_w_qkv': _L0_attn_in['w_qkv'], 'L0_attn_w_dense': _L0_attn_in['w_dense'], 'L0_ffn_up': _L0_ffn_in['up'], 'L0_ffn_down': _L0_ffn_in['down'], 'L0_ffn_perm': _L0_ffn_in['perm']}

def reference(x, L0_tok_kernel, L0_tok_bias, L0_tok_pos_emb, L0_attn_w_qkv, L0_attn_w_dense, L0_ffn_up, L0_ffn_down, L0_ffn_perm):
    import jax
    import jax.numpy as jnp

    def _L0_tok_ref(x, kernel, bias, pos_emb):
        import jax, jax.numpy as jnp
        import numpy as np
        SHARDS = 8
        VOCAB = 12600
        VS = VOCAB // SHARDS
        D = 1024
        SEQ = 512
        B = 4
        shards, vs, d = kernel.shape
        starts = jnp.arange(shards, dtype=x.dtype) * vs

        def step(acc, shard):
            start, W = shard
            idx = jnp.clip(x - start, 0, vs - 1)
            return (acc + W[idx], None)
        acc0 = jnp.zeros(x.shape + (d,), kernel.dtype)
        out, _ = jax.lax.scan(step, acc0, (starts, kernel))
        out = out + shards * bias + pos_emb
        return out

    def _L0_attn_ref(q, w_qkv, w_dense):
        import jax, jax.numpy as jnp
        import numpy as np
        B, S, EMB = (2, 512, 1024)
        NHEADS, KVHEADS, HEAD_D = (32, 8, 128)
        SPLITS = (NHEADS * HEAD_D, KVHEADS * HEAD_D, KVHEADS * HEAD_D)
        Bq, Sq, _ = q.shape
        qkv = q @ w_qkv.T
        qs, ks, vs = jnp.split(qkv, np.cumsum(SPLITS)[:-1], axis=-1)
        G = NHEADS // KVHEADS
        qh = qs.reshape(Bq, Sq, KVHEADS, G, HEAD_D)
        kh = ks.reshape(Bq, Sq, KVHEADS, HEAD_D)
        vh = vs.reshape(Bq, Sq, KVHEADS, HEAD_D)
        scale = 1.0 / jnp.sqrt(jnp.float32(HEAD_D))
        scores = jnp.einsum('bskgd,btkd->bkgst', qh, kh) * scale
        causal = jnp.tril(jnp.ones((Sq, Sq), dtype=bool))
        scores = jnp.where(causal, scores, jnp.finfo(scores.dtype).min)
        probs = jax.nn.softmax(scores, axis=-1)
        attn = jnp.einsum('bkgst,btkd->bskgd', probs, vh)
        attn = attn.reshape(Bq, Sq, NHEADS * HEAD_D)
        return attn @ w_dense.T

    def _L0_ffn_ref(x, up, down, perm):
        import jax, jax.numpy as jnp
        import numpy as np
        B, L, H, Dh, M = (4, 512, 16, 64, 256)
        D = H * Dh
        b, l, Dm = x.shape
        h, d = (up.shape[0], up.shape[1])
        unperm = jnp.argsort(perm)
        t = x.reshape(b * l, Dm)
        t = t[:, perm]
        t = t.reshape(b * l, h, d)
        t = jnp.einsum('bhd,hdm->bhm', t, up)
        t = jax.nn.gelu(t, approximate=False)
        t = jnp.einsum('bhm,hmd->bhd', t, down)
        t = t.reshape(b * l, h * d)
        t = t[:, unperm]
        out = t.reshape(b, l, Dm)
        return out
    h = _L0_tok_ref(x, L0_tok_kernel, L0_tok_bias, L0_tok_pos_emb)
    h = h + _L0_attn_ref(_layernorm(h, axis=-1), L0_attn_w_qkv, L0_attn_w_dense)
    h = h + _L0_ffn_ref(_layernorm(h, axis=-1), L0_ffn_up, L0_ffn_down, L0_ffn_perm)
    return h

_drawn_inputs = setup_inputs


def setup_inputs(seed=0):
    import zlib

    import numpy as np

    out = dict(_drawn_inputs(seed))
    spreads = {'L0_tok_bias': (0.0, 0.1)}
    factors = {'L0_tok_pos_emb': 3.367}
    for name, (base, spread) in spreads.items():
        noise = np.random.default_rng([zlib.crc32(name.encode()), seed]).standard_normal(out[name].shape)
        drawn = base * np.exp(spread * noise) if base else spread * noise
        out[name] = jnp.asarray(drawn.astype(out[name].dtype))
    for name, factor in factors.items():
        out[name] = (out[name] * factor).astype(out[name].dtype)
    return out
```

```python
from contextlib import ExitStack

import concourse.bass as bass
from concourse import mybir

F32 = mybir.dt.float32
F32R = mybir.dt.float32r
BF16 = mybir.dt.bfloat16
I32 = mybir.dt.int32
U32 = mybir.dt.uint32
ALU = mybir.AluOpType
ACT = mybir.ActivationFunctionType

P = 128
B, S, E = 4, 512, 1024
G, HQ, D = 8, 4, 128
KT = E // P
TT = S // P
SHARDS, VS = 8, 1575
VOCAB = SHARDS * VS
HEADS, DH, MH = 16, 64, 256
PAIRS = HEADS // 2
EDGE = 2 * (SHARDS - 1) + 1
SCALE = float(D) ** -0.5
EPS = 1e-5
LOWEST = -3.0e38

RQ, RD, RF = 3, 4, 2
QKV_TILES = G * (HQ + 2)

P_OFF = [0, 128, 384, 768]
P_LEN = 1280
SC_AT = [(0, 0), (0, 256), (1, 0), (2, 0)]
PT_OFF = [0, 512, 896]
PT_LEN = 1152

MID = ("S0 Q2 N0 D0 Ta0 D1 Tb0 S1 Q3 N1 D2 Ta1 D3 Tb1 S2 D4 D5 N2 D6 D7 PV0 "
       "Ta2 Q0 Tb2 S3 PV1 K N3 Q1 Ta3 PV2 Tb3 V PV3 VT").split()
FIRST = [s.replace("D", "H") if s[0] == "D" else s for s in MID]
FIRST.insert(FIRST.index("H7") + 1, "G")
LAST = ("S0 Q2 N0 D0 Ta0 D1 Tb0 S1 Q3 N1 D2 Ta1 D3 Tb1 A0 S2 D4 D5 A1 N2 D6 B0 B1 A2 D7 PV0 "
        "Ta2 B2 B3 A3 Tb2 S3 B4 B5 PV1 B6 B7 N3 L Ta3 PV2 X0 X1 Tb3 X2 X3 PV3 X4 X5 X6 X7").split()
LAST_ALONE = [s for s in LAST if s[0] not in "ABXL"]
POST = "D0 D1 D2 D3 D4 D5 D6 D7 ST Q0 K Q1 M V VT R F".split()
POST_ALONE = "D0 D1 D2 D3 D4 D5 D6 D7 ST M R F".split()
START = "G A0 B0 B1 A1 B2 B3 A2 B4 B5 A3 B6 B7 L X0 X1 X2 X3 X4 X5 X6 X7 Q0 K Q1 V VT".split()


def is_job(s):
    return s[0] in "QKDHBX" or s == "V"


def number(steps, which):
    out, n = {}, 0
    for s in steps:
        if which(s):
            out[s] = n
            n += 1
    return out


def is_qkv(s):
    return s[0] in "QK" or s == "V"


def is_split_job(s):
    return s[0] in "QKX"


class Place:

    def __init__(self, steps, b, g, kind):
        self.b, self.g, self.steps, self.kind = b, g, steps, kind
        self.n = 8 * b + g
        if kind == "start":
            self.half, self.split, self.wq = 0, 0, 0
        elif kind == "post":
            self.half, self.split, self.wq = 72 + 84 * b, 11 + 48 * b + 45, 4 + 48 * b + 44
            if "Q0" not in steps:
                self.half -= 8
        else:
            self.half, self.split, self.wq = 10 + 84 * b + 7 * g, 11 + 48 * b + 5 * g, 4 + 48 * b + 6 * g
        self.wd = 64 * b + 56 if kind == "post" else 64 * b + 8 * (g - 1)
        self.wq_tile = 0 if kind in ("start", "post") else 4 + 6 * g
        self.wd_tile = 56 if kind == "post" else 8 * (g - 1)
        self.jobs = number(steps, is_job)
        self.splits = number(steps, is_split_job)
        self.weights = number(steps, is_qkv)

    def bank(self, s):
        return self.jobs[s] % 2

    def full(self, s):
        return 2 * self.half + (self.jobs[s] + 1)

    def free(self, s):
        return self.half + self.jobs[s] // 2

    def split_done(self, s):
        return self.split + (self.splits[s] + 1)

    def wq_at(self, s):
        return self.wq + self.weights[s]

    def wq_slot(self, s, n, ahead=0):
        first = {"start": 0, "post": 48}.get(self.kind, 4)
        return (first + self.weights[s] + ahead) % n


def tower_kernel(nc, x_cols, x_row, table, bias, pos, edge_cols, w_qkv, w_dense, w_mlp, perm_cols, out):
    scratch = nc.dram_tensor("h1_rows", [E, S], F32).ap()
    ctx = ExitStack()
    with ctx:
        def sb(name, shape, dt, at=ctx):
            return at.enter_context(nc.sbuf_tensor(name, shape, dt))

        def ps(name, shape, dt=F32):
            return ctx.enter_context(nc.psum_tensor(name, shape, dt))

        def sem(name):
            return ctx.enter_context(nc.semaphore(name))

        xn_hi = sb("xn_hi", [P, KT, S], F32R)
        xn_lo = sb("xn_lo", [P, KT, S], F32R)
        h_tok = sb("h_tok", [P, TT, E], F32)
        row_buf = sb("row_buf", [P, E], F32)
        hacc = sb("hacc", [P, KT, S], F32)
        wq_raw = sb("wq_raw", [P, 2, E], F32)
        wq_hi = sb("wq_hi", [P, RQ, E], F32R)
        wq_lo = sb("wq_lo", [P, RQ, E], F32R)
        wd_raw = sb("wd_raw", [P, 2, HQ * P], F32)
        wd_hi = sb("wd_hi", [P, RD, HQ * P], F32R)
        wd_lo = sb("wd_lo", [P, RD, HQ * P], F32R)
        q_hi = sb("q_hi", [P, 2, S], F32R)
        q_lo = sb("q_lo", [P, 2, S], F32R)
        k_hi = sb("k_hi", [P, S], F32R)
        k_lo = sb("k_lo", [P, S], F32R)
        v_hi = sb("v_hi", [P, TT, D], F32R)
        v_lo = sb("v_lo", [P, TT, D], F32R)
        v_feat = sb("v_feat", [P, S], F32)
        pt3_hi = sb("pt3_hi", [P, 2, 256], F32R)
        pt3_lo = sb("pt3_lo", [P, 2, 256], F32R)
        mask = sb("mask", [P, S], F32)
        ident = sb("ident", [P, P], F32)
        ones = sb("ones", [P, P], F32R)
        edges = sb("edges", [96, E], BF16)
        coef = sb("coef", [96, S], BF16)
        coef_all = sb("coef_all", [96, B * S], BF16)
        edge_consts = sb("edge_consts", [96, 3], F32)
        xi = sb("xi", [P, B * TT], I32)
        rows_all = sb("rows_all", [P, B * TT], I32)
        rows_now = sb("rows_now", [P, TT], I32)
        perm = sb("perm", [P, KT], I32)
        perm_now = sb("perm_now", [P, KT], I32)
        stats = sb("stats", [P, TT, 2, 6], F32)
        moments = sb("moments", [P, TT, 2], F32)
        var_eps = sb("var_eps", [P, TT], F32)
        inv_var = sb("inv_var", [P, TT], F32)
        rstd = sb("rstd", [P, TT], F32)
        shift = sb("shift", [P, TT], F32)
        row_max = sb("row_max", [P, TT], F32)
        neg_max = sb("neg_max", [P, TT], F32)
        row_sum = sb("row_sum", [P, TT], F32)
        inv_sum = sb("inv_sum", [P, TT], F32)
        up_hi = sb("up_hi", [P, RF, 2, MH], F32R)
        up_lo = sb("up_lo", [P, RF, 2, MH], F32R)
        dn_hi = sb("dn_hi", [P, RF, 4, P], F32R)
        dn_lo = sb("dn_lo", [P, RF, 4, P], F32R)

        with ExitStack() as own:
            at_hi = sb("at_hi", [P, HQ, S], F32R, own)
            at_lo = sb("at_lo", [P, HQ, S], F32R, own)
            pt_hi = sb("pt_hi", [P, 2, PT_LEN], F32R, own)
            pt_lo = sb("pt_lo", [P, 2, PT_LEN], F32R, own)
            prob = sb("prob", [P, P_LEN], F32, own)
        with ExitStack() as own:
            g_hi = sb("g_hi", [P, 2, 2, S], F32R, own)
            g_lo = sb("g_lo", [P, 2, 2, S], F32R, own)
            g_raw = sb("g_raw", [P, 2, S], F32, own)
            y_hi = sb("y_hi", [P, 2, S], F32R, own)
            y_lo = sb("y_lo", [P, 2, S], F32R, own)
            y_raw = sb("y_raw", [P, S], F32, own)
            mean2 = sb("mean2", [P, S], F32, own)
            rstd2 = sb("rstd2", [P, S], F32, own)
            wf_raw = sb("wf_raw", [P, 2, 2 * MH], F32, own)
        sc = ps("sc", [P, 3, S])
        tp = ps("tp", [P, 2, S])
        pv = ps("pv", [P, S])
        fb = ps("fb", [P, 2, S])

        const_in = sem("const_in")
        edge_in = sem("edge_in")
        edge_step = sem("edge_step")
        zeroed = sem("zeroed")
        selected = sem("selected")
        rows_ready = sem("rows_ready")
        gathered = sem("gathered")
        pos_in = sem("pos_in")
        pos_added = sem("pos_added")
        h_step = sem("h_step")
        rstd_done = sem("rstd_done")
        row_ready = sem("row_ready")
        job_full = sem("job_full")
        bank_free = [sem("bank0_free"), sem("bank1_free")]
        split_hi = sem("split_hi")
        wq_in = [sem("wq_in0"), sem("wq_in1")]
        wq_rounded = sem("wq_rounded")
        wq_ready = sem("wq_ready")
        wd_in = [sem("wd_in0"), sem("wd_in1")]
        wd_rounded = sem("wd_rounded")
        wd_ready = sem("wd_ready")
        wf_in = [sem("wf_in0"), sem("wf_in1")]
        wf_rounded = sem("wf_rounded")
        wf_ready = sem("wf_ready")
        up_ready = sem("up_ready")
        tp_full = sem("tp_full")
        tp_hi = sem("tp_hi")
        tpa_free = sem("tpa_free")
        tpb_free = sem("tpb_free")
        sc_full = sem("sc_full")
        tile_max = sem("tile_max")
        max_ready = sem("max_ready")
        exp_done = sem("exp_done")
        inv_ready = sem("inv_ready")
        prob_ready = sem("prob_ready")
        pv_full = sem("pv_full")
        at_rounded = sem("at_rounded")
        pv_free = sem("pv_free")
        stored = sem("stored")
        turned = sem("turned")
        y_rounded = sem("y_rounded")
        y_ready = sem("y_ready")
        y_step = sem("y_step")
        squared = sem("squared")
        stat_full = sem("stat_full")
        rstd2_done = sem("rstd2_done")
        perm_ready = sem("perm_ready")
        g_rounded = sem("g_rounded")
        g_low_pool = sem("g_low_pool")
        g_low_dve = sem("g_low_dve")
        scattered = sem("scattered")
        hacc_free = sem("hacc_free")
        apart = sem("apart")

        block = ctx.enter_context(nc.Block())

        def walk(eng, stage):
            stage(Place(START, 0, 0, "start"))

            def batch(b, last):
                stage(Place(FIRST if not last else [s for s in FIRST if s != "G"], b, 0, "first"))
                with eng.Fori(1, G - 1) as g:
                    stage(Place(MID, b, g, "mid"))
                stage(Place(LAST_ALONE if last else LAST, b, G - 1, "last"))
                stage(Place(POST_ALONE if last else POST, b, 0, "post"))

            with eng.Fori(0, B - 1) as b:
                batch(b, False)
            batch(B - 1, True)

        @block.sync
        def _(sp):
            sp.dma_start(xi[:, :], x_cols).then_inc(const_in, 16)
            sp.dma_start(perm[:, :], perm_cols).then_inc(const_in, 16)
            for part in range(3):
                at = slice(32 * part, 32 * part + 32)
                sp.dma_start(edge_consts[at, :], edge_cols).then_inc(const_in, 16)
                sp.dma_start(h_tok[at, 0:2, :].rearrange("p a n -> p (a n)").bitcast(I32),
                             x_row.partition_broadcast(32)).then_inc(const_in, 16)
            sp.wait_ge(zeroed, 1)
            shards = table.rearrange("(s v) e -> s v e", v=VS)
            for part in range(3):
                at = 32 * part
                n = SHARDS - 1
                sp.dma_start(row_buf[at:at + n, :], shards[0:n, VS - 1, :]).then_inc(edge_in, 16)
                sp.dma_start(row_buf[at + n:at + 2 * n, :], shards[1:SHARDS, 0, :]).then_inc(edge_in, 16)
                sp.dma_start(row_buf[at + 2 * n:at + EDGE, :], bias).then_inc(edge_in, 16)

            def load_wq(slot, index):
                sp.dma_start(wq_raw[:, slot, :], w_qkv[index]).then_inc(wq_in[slot], 16)

            for m in range(RQ):
                if m >= 2:
                    sp.wait_ge(wq_ready, m - 1)
                load_wq(m % 2, m)

            def load_wd(place, m):
                sp.wait_ge(wd_ready, place.wd + (m + 1))
                sp.dma_start(wd_raw[:, m % 2, :], w_dense[place.wd_tile + m]).then_inc(wd_in[m % 2], 16)

            def stage(place):
                b = place.b
                if place.kind == "first":
                    for m in range(RD):
                        sp.wait_ge(wd_ready, 64 * b + (m + 1))
                        sp.dma_start(wd_raw[:, m % 2, :], w_dense[m]).then_inc(wd_in[m % 2], 16)
                for s in place.steps:
                    if is_qkv(s):
                        if "X0" not in place.steps and place.kind == "last":
                            continue
                        k = place.weights[s] + RQ
                        sp.wait_ge(wq_ready, place.wq + (k - 1))
                        load_wq(place.wq_slot(s, 2, RQ), place.wq_tile + k)
                    if s[0] == "D" and not (place.kind == "post" and int(s[1]) >= RD):
                        load_wd(place, int(s[1]) + RD)
                    if s[0] == "A":
                        c = int(s[1])
                        done = 4 * (b + 1) if place.kind != "start" else 0
                        if c > 0:
                            sp.wait_ge(pos_added, done + c)
                        elif place.kind == "start":
                            sp.wait_ge(edge_step, 7)
                        else:
                            sp.wait_ge(job_full, place.full("D0"))
                        sp.dma_start(row_buf[:, :], pos[c * P:(c + 1) * P, :]).then_inc(pos_in, 16)
                    if s == "ST":
                        sp.wait_ge(bank_free[1], place.half + 4)
                        sp.wait_ge(bank_free[0], place.half + 4)
                        sp.dma_start(scratch.rearrange("(k p) n -> p k n", p=P),
                                     hacc[:, :, :]).then_inc(stored, 16)
                    if s == "F":
                        for p in range(PAIRS):
                            sp.wait_ge(wf_ready, 8 * b + (p + 1))
                            sp.dma_start(wf_raw[:, p % 2, :], w_mlp[p]).then_inc(wf_in[p % 2], 16)

            walk(sp, stage)

        @block.tensor
        def _(pe):
            def product(dst, a_hi, a_lo, b_hi, b_lo, first, last):
                pe.matmul(dst, a_hi, b_hi, start=first, stop=False)
                pe.matmul(dst, a_hi, b_lo, start=False, stop=False)
                return pe.matmul(dst, a_lo, b_hi, start=False, stop=last)

            def scores(place, i):
                n, q = place.n, i % 2
                if i == 0:
                    pe.wait_ge(bank_free[0], place.half - 1)
                    pe.wait_ge(bank_free[1], place.half - 1)
                if i == 1:
                    pe.wait_ge(bank_free[0], place.half)
                if i == 2:
                    pe.wait_ge(bank_free[place.bank("Q2")], place.free("Q2") + 1)
                if i == 3:
                    pe.wait_ge(bank_free[place.bank("Q3")], place.free("Q3") + 1)
                for t in range(TT):
                    bank, c = SC_AT[t]
                    w = max(256, P * (t + 1))
                    qt = slice(t * P, (t + 1) * P)
                    mm = product(sc[:, bank, c:c + w], q_hi[:, q, qt], q_lo[:, q, qt],
                                 k_hi[:, 0:w], k_lo[:, 0:w], True, True)
                    if t > 0:
                        mm.then_inc(sc_full, 1)

            def turn(place, i, part):
                def block_(bank, c, t, j):
                    return pe.transpose(tp[:, bank, c:c + P], prob[:, P_OFF[t] + j * P:P_OFF[t] + (j + 1) * P],
                                        ident[:, :])
                n = place.n
                if part == "a":
                    pe.wait_ge(prob_ready, 16 * n + (4 * i + 4))
                    pe.wait_ge(tpa_free, 9 * n + (2 * i + 1))
                    for t in range(TT):
                        last = block_(0, t * P, t, 0)
                    last.then_inc(tp_full, 1)
                    pe.wait_ge(tpb_free, 5 * n + (i + 1))
                    for t in range(1, TT):
                        block_(1, (t - 1) * P, t, 1)
                    block_(1, 3 * P, 3, 3).then_inc(tp_full, 1)
                else:
                    pe.wait_ge(tpa_free, 9 * n + (2 * i + 2))
                    block_(0, 0, 2, 2)
                    block_(0, P, 3, 2).then_inc(tp_full, 1)

            def values(place, i):
                n, r = place.n, i % 2
                pe.wait_ge(tpa_free, 9 * n + (2 * i + 3))
                pe.wait_ge(pv_free, 40 * place.b + 4 * place.g + (i + 1))
                for j in range(TT):
                    if j < 3:
                        cols = slice(j * P, S)
                        at = slice(PT_OFF[j], PT_OFF[j] + S - j * P)
                        b_hi, b_lo = pt_hi[:, r, at], pt_lo[:, r, at]
                    else:
                        cols = slice(S - 256, S)
                        b_hi, b_lo = pt3_hi[:, r, :], pt3_lo[:, r, :]
                    mm = product(pv[:, cols], v_hi[:, j, :], v_lo[:, j, :], b_hi, b_lo, j == 0, j == 3)
                mm.then_inc(pv_full, 1)

            def start_job(place, s):
                if not (place.kind == "start" and place.jobs[s] < 2):
                    pe.wait_ge(bank_free[place.bank(s)], place.free(s))
                return fb[:, place.bank(s), :]

            def project(place, s):
                slot = place.wq_slot(s, RQ)
                pe.wait_ge(wq_ready, place.wq_at(s) + 1)
                dst = start_job(place, s)
                for k in range(KT):
                    w = slice(k * P, (k + 1) * P)
                    mm = product(dst, wq_hi[:, slot, w], wq_lo[:, slot, w], xn_hi[:, k, :], xn_lo[:, k, :],
                                 k == 0, k == KT - 1)
                mm.then_inc(job_full, 1)

            def dense(place, s):
                m = int(s[1])
                if m == 0:
                    pe.wait_ge(pv_free, 40 * place.b + (33 if place.kind == "post" else 4 * place.g + 1))
                pe.wait_ge(wd_ready, place.wd + (m + 3))
                dst = start_job(place, s)
                for h in range(HQ):
                    w = slice(h * P, (h + 1) * P)
                    mm = product(dst, wd_hi[:, m % RD, w], wd_lo[:, m % RD, w], at_hi[:, h, :], at_lo[:, h, :],
                                 h == 0, h == HQ - 1)
                mm.then_inc(job_full, 1)

            def stage(place):
                b = place.b
                for s in place.steps:
                    k = int(s[-1]) if s[-1].isdigit() else 0
                    if s[0] == "S" and s != "ST":
                        scores(place, k)
                    elif s[:2] in ("Ta", "Tb"):
                        turn(place, k, s[1])
                    elif s[:2] == "PV":
                        values(place, k)
                    elif is_qkv(s):
                        if place.kind == "start" and s == "Q0":
                            pe.wait_ge(bank_free[0], 8)
                            pe.wait_ge(bank_free[1], 8)
                        project(place, s)
                    elif s[0] == "D":
                        dense(place, s)
                    elif s[0] == "H":
                        c, half = k // 2, k % 2
                        dst = start_job(place, s)
                        for j in range(4):
                            f = (4 * half + j) * P
                            mm = pe.transpose(dst[:, j * P:(j + 1) * P], h_tok[:, c, f:f + P], ident[:, :])
                        mm.then_inc(job_full, 1)
                    elif s[0] == "B":
                        c, half = k // 2, k % 2
                        if k == 0:
                            pe.wait_ge(rows_ready, 2 if place.kind == "start" else 2 * b + 4)
                            pe.wait_ge(edge_step, 10)
                        dst = start_job(place, s)
                        pe.matmul(dst, coef[:, c * P:(c + 1) * P], edges[:, half * S:(half + 1) * S],
                                  start=True, stop=True).then_inc(job_full, 1)
                    elif s[0] == "X":
                        c, half = k // 2, k % 2
                        done = 0 if place.kind == "start" else 4 * (b + 1)
                        pe.wait_ge(row_ready, done + (c + 1))
                        dst = start_job(place, s)
                        for j in range(4):
                            f = (4 * half + j) * P
                            mm = pe.transpose(dst[:, j * P:(j + 1) * P], row_buf[:, f:f + P], ident[:, :])
                        mm.then_inc(job_full, 1)
                    elif s == "VT":
                        n = 0 if place.kind == "start" else (place.n + 1 if place.kind != "post" else 8 * b + 8)
                        pe.wait_ge(bank_free[place.bank("V")], place.free("V") + 1)
                        if place.kind != "start":
                            pe.wait_ge(tpa_free, 9 * n)
                            pe.wait_ge(tpb_free, 5 * n)
                        for j in range(TT):
                            mm = pe.transpose(tp[:, j // 2, (j % 2) * P:(j % 2 + 1) * P],
                                              v_feat[:, j * P:(j + 1) * P], ident[:, :])
                            if j % 2:
                                mm.then_inc(tp_full, 1)
                    elif s in "MR":
                        bank = 1 if s == "M" else 2
                        base = 24 * b + (0 if s == "M" else 8)
                        for j in range(KT):
                            pe.wait_ge(y_ready, base + (j + 1))
                            pe.matmul(sc[:, bank, :], ones[:, :], y_hi[:, j % 2, :], start=j == 0, stop=False)
                            mm = pe.matmul(sc[:, bank, :], ones[:, :], y_lo[:, j % 2, :], start=False, stop=j == KT - 1)
                            mm.then_inc(stat_full, 1)
                    elif s == "F":
                        mlp(place)

            def mlp(place):
                b = place.b
                first_job = len(place.jobs)
                for hh in range(HEADS + 1):
                    if hh < HEADS:
                        p, h = hh // 2, hh % 2
                        if h == 0:
                            pe.wait_ge(wf_ready, 8 * b + (p + 3))
                            pe.wait_ge(y_ready, 24 * b + (16 + p + 1))
                        for kt in range(2):
                            job = first_job + 2 * hh + kt
                            pe.wait_ge(bank_free[job % 2], place.half + job // 2)
                            cols = slice(kt * P, (kt + 1) * P)
                            product(fb[:, job % 2, :], up_hi[:, p % 2, h, cols], up_lo[:, p % 2, h, cols],
                                    y_hi[:, p % 2, :], y_lo[:, p % 2, :], True, True).then_inc(job_full, 1)
                    if hh > 0:
                        p, h = (hh - 1) // 2, (hh - 1) % 2
                        pe.wait_ge(g_low_pool, 16 * b + hh)
                        pe.wait_ge(g_low_dve, 16 * b + hh)
                        if h == 0:
                            pe.wait_ge(pv_free, 40 * b + (33 + p))
                        for kt in range(2):
                            w = 2 * h + kt
                            mm = product(pv[:, :], dn_hi[:, p % 2, w, :], dn_lo[:, p % 2, w, :],
                                         g_hi[:, h, kt, :], g_lo[:, h, kt, :], w == 0, w == 3)
                        if h == 1:
                            mm.then_inc(pv_full, 1)

            pe.wait_ge(zeroed, 8)
            pe.wait_ge(selected, 2)
            walk(pe, stage)

        @block.scalar
        def _(act):
            copy = ACT.Copy

            def split_wq(place, k):
                first = {"start": 0, "post": 48}.get(place.kind, 4)
                raw, slot = (first + k) % 2, (first + k) % RQ
                act.wait_ge(wq_in[raw], 16 * half_up(place, k))
                act.activation(wq_hi[:, slot, :], wq_raw[:, raw, :], copy).then_inc(wq_rounded, 1)

            def half_up(place, k):
                base = {"start": 0, "post": 24 + 24 * place.b}.get(place.kind, 2 + 24 * place.b + 3 * place.g)
                return base + (k // 2 + 1)

            def split_wd(place, m):
                base = 32 * place.b + (28 if place.kind == "post" else 4 * (place.g - 1))
                act.wait_ge(wd_in[m % 2], 16 * (base + (m // 2 + 1)))
                act.activation(wd_hi[:, m % RD, :], wd_raw[:, m % 2, :], copy).then_inc(wd_rounded, 1)

            def split_wf(b, p):
                r = p % 2
                act.wait_ge(wf_in[r], 16 * (4 * b + (p // 2 + 1)))
                for h in range(2):
                    rows = slice(h * DH, (h + 1) * DH)
                    act.activation(up_hi[rows, r, h, :], wf_raw[rows, r, 0:MH], copy)
                    act.activation(dn_hi[:, r, 2 * h:2 * h + 2, rows],
                                   wf_raw[:, r, MH + h * P:MH + (h + 1) * P].rearrange("p (k d) -> p k d", k=2),
                                   copy).then_inc(wf_rounded, 1)

            def stage(place):
                b, n = place.b, place.n
                if place.kind == "first":
                    for m in range(RD):
                        act.wait_ge(wd_in[m % 2], 16 * (32 * b + (m // 2 + 1)))
                        act.activation(wd_hi[:, m % RD, :], wd_raw[:, m % 2, :], copy).then_inc(wd_rounded, 1)
                for s in place.steps:
                    i = int(s[-1]) if s[-1].isdigit() else 0
                    if s[0] == "S" and s != "ST":
                        act.wait_ge(max_ready, 4 * n + (i + 1))
                        for t in range(TT):
                            bank, c = SC_AT[t]
                            w = P * (t + 1)
                            act.activation(prob[:, P_OFF[t]:P_OFF[t] + w], sc[:, bank, c:c + w], ACT.Exp,
                                           bias=neg_max[:, t:t + 1], scale=SCALE,
                                           accum_out=row_sum[:, t:t + 1]).then_inc(exp_done, 1)
                    elif s[:2] == "Ta":
                        r = i % 2
                        act.wait_ge(tp_full, 14 * n + (3 * i + 3))
                        act.activation(pt_hi[:, r, 0:S], tp[:, 0, :], copy).then_inc(tp_hi, 1)
                        act.wait_ge(tp_full, 14 * n + (3 * i + 4))
                        act.activation(pt_hi[:, r, S:S + 384], tp[:, 1, 0:384], copy).then_inc(tp_hi, 1)
                        act.activation(pt3_hi[:, r, P:2 * P], tp[:, 1, 384:S], copy).then_inc(tp_hi, 1)
                    elif s[:2] == "Tb":
                        act.wait_ge(tp_full, 14 * n + (3 * i + 5))
                        act.activation(pt_hi[:, i % 2, 896:PT_LEN], tp[:, 0, 0:256], copy).then_inc(tp_hi, 1)
                    elif s[:2] == "PV":
                        act.wait_ge(pv_full, 40 * b + 4 * place.g + (i + 1))
                        act.activation(at_hi[:, i, :], pv[:, :], copy).then_inc(at_rounded, 1)
                    elif s[0] in "QK":
                        act.wait_ge(job_full, place.full(s))
                        dst = k_hi[:, :] if s == "K" else q_hi[:, i % 2, :]
                        act.activation(dst, fb[:, place.bank(s), :], copy).then_inc(split_hi, 1)
                    elif s == "V":
                        act.wait_ge(job_full, place.full(s))
                        act.activation(v_feat[:, :], fb[:, place.bank(s), :], copy)\
                           .then_inc(bank_free[place.bank(s)], 1)
                    elif s == "VT":
                        base = 0 if place.kind == "start" else (14 * n + 14 if place.kind != "post" else 14 * (8 * b + 8))
                        for half in range(2):
                            act.wait_ge(tp_full, base + (half + 1))
                            act.activation(v_hi[:, 2 * half:2 * half + 2, :],
                                           tp[:, half, 0:256].rearrange("p (j d) -> p j d", j=2), copy)\
                               .then_inc(tp_hi, 1)
                    elif s[0] == "H":
                        c, half = i // 2, i % 2
                        if i == 0:
                            act.wait_ge(hacc_free, b + 1)
                        act.wait_ge(job_full, place.full(s))
                        act.activation(hacc[:, 4 * half:4 * half + 4, c * P:(c + 1) * P],
                                       fb[:, place.bank(s), :].rearrange("p (j t) -> p j t", j=4), copy)\
                           .then_inc(bank_free[place.bank(s)], 1)
                    elif s == "L":
                        done = 1 if place.kind == "start" else b + 2
                        act.wait_ge(h_step, 15 * done - 1)
                        act.activation(rstd[:, :], inv_var[:, :], ACT.Sqrt).then_inc(rstd_done, 1)
                        act.wait_ge(h_step, 15 * done)
                    elif s[0] == "X":
                        c, half = i // 2, i % 2
                        if half == 0:
                            if c > 0:
                                act.wait_ge(job_full, place.full(f"X{i - 1}"))
                            act.activation(row_buf[:, :], h_tok[:, c, :], ACT.Identity,
                                           scale=rstd[:, c:c + 1], bias=shift[:, c:c + 1]).then_inc(row_ready, 1)
                        act.wait_ge(job_full, place.full(s))
                        act.activation(xn_hi[:, 4 * half:4 * half + 4, c * P:(c + 1) * P],
                                       fb[:, place.bank(s), :].rearrange("p (j t) -> p j t", j=4), copy)\
                           .then_inc(split_hi, 1)
                    elif s == "M":
                        act.wait_ge(turned, 128 * (b + 1))
                        for j in range(KT):
                            if j >= 2:
                                act.wait_ge(stat_full, 16 * b + (j - 1))
                            act.activation(y_hi[:, j % 2, :], hacc[:, j, :], copy).then_inc(y_rounded, 1)
                    elif s == "R":
                        for j in range(KT):
                            act.wait_ge(y_step, 27 * b + (j + 2))
                            act.wait_ge(stat_full, 16 * b + (8 + j - 1))
                            act.activation(g_raw[:, j % 2, :], y_raw[:, :], ACT.Square).then_inc(squared, 1)
                            act.wait_ge(squared, 8 * b + (j + 1))
                            act.activation(y_hi[:, j % 2, :], g_raw[:, j % 2, :], copy).then_inc(y_rounded, 1)
                        act.wait_ge(y_step, 27 * b + 11)
                        act.activation(rstd2[:, :], y_raw[:, :], ACT.Sqrt).then_inc(rstd2_done, 1)
                    elif s == "F":
                        mlp(place)
                    if is_qkv(s) and not (place.kind == "last" and "X0" not in place.steps):
                        split_wq(place, place.weights[s] + RQ)
                    if s[0] == "D" and not (place.kind == "post" and i >= RD):
                        act.wait_ge(job_full, place.full(s))
                        split_wd(place, i + RD)

            def mlp(place):
                b = place.b
                first_job = len(place.jobs)
                split_wf(b, 0)
                split_wf(b, 1)

                def input_hi(p):
                    act.wait_ge(y_step, 27 * b + (13 + 2 * p))
                    if p < 2:
                        act.wait_ge(stat_full, 16 * b + 16)
                    act.activation(y_hi[:, p % 2, :], y_raw[:, :], copy).then_inc(y_rounded, 1)

                input_hi(0)
                for hh in range(HEADS):
                    p, h = hh // 2, hh % 2
                    for kt in range(2):
                        job = first_job + 2 * hh + kt
                        act.wait_ge(job_full, 2 * place.half + (job + 1))
                        if hh > 0:
                            act.wait_ge(g_low_pool if kt == 0 else g_low_dve, 16 * b + hh)
                        act.activation(g_raw[:, kt, :], fb[:, job % 2, :], ACT.Gelu)\
                           .then_inc(bank_free[job % 2], 1)
                    if h == 0 and p + 1 < PAIRS:
                        input_hi(p + 1)
                    if h == 0 and 1 <= p < PAIRS - 1:
                        act.wait_ge(pv_full, 40 * b + (32 + p))
                        split_wf(b, p + 1)

            for m in range(RQ):
                act.wait_ge(wq_in[m % 2], 16 * (m // 2 + 1))
                act.activation(wq_hi[:, m, :], wq_raw[:, m % 2, :], copy).then_inc(wq_rounded, 1)
            walk(act, stage)

        @block.vector
        def _(dve):
            dve.memset(row_buf[:, :], 0.0).then_inc(zeroed, 1)
            for t, value in ((mask[:, :], 0.0), (ident[:, :], 0.0), (ones[:, :].bitcast(F32), 1.0),
                             (up_hi[:, :, :, :].bitcast(F32), 0.0), (up_lo[:, :, :, :].bitcast(F32), 0.0),
                             (dn_hi[:, :, :, :].bitcast(F32), 0.0), (dn_lo[:, :, :, :].bitcast(F32), 0.0)):
                dve.memset(t, value).then_inc(zeroed, 1)
            dve.memset(pt3_hi[:, :, :].bitcast(F32), 0.0).then_inc(zeroed, 1)
            dve.memset(pt3_lo[:, :, :].bitcast(F32), 0.0).then_inc(pv_free, 1)

            dve.wait_ge(const_in, 128)
            dve.wait_ge(edge_in, 144)
            steps = [0]

            def step(ins):
                ins.then_inc(edge_step, 1)
                steps[0] += 1
                dve.wait_ge(edge_step, steps[0])
            rows = row_buf[0:96, :]
            step(dve.tensor_scalar(rows, rows, edge_consts[:, 2:3], None, ALU.mult))
            step(dve.tensor_copy(edges[:, :], rows))
            step(dve.tensor_tensor(rows, rows, edges[:, :], ALU.subtract))
            step(dve.tensor_copy(edges[32:64, :], row_buf[32:64, :]))
            step(dve.tensor_copy(edges[64:96, :], row_buf[64:96, :]))
            step(dve.tensor_tensor(row_buf[64:96, :], row_buf[64:96, :], edges[64:96, :], ALU.subtract))
            step(dve.tensor_copy(edges[64:96, :], row_buf[64:96, :]))
            step(dve.tensor_scalar(coef_all[:, :], h_tok[0:96, 0:2, :].rearrange("p a n -> p (a n)").bitcast(I32),
                                   edge_consts[:, 0:1], edge_consts[:, 1:2], ALU.mult, ALU.is_ge))
            step(dve.tensor_scalar(rows_all[:, :], xi[:, :], 0, VOCAB - 1, ALU.max, ALU.min))
            step(dve.tensor_scalar(perm_now[:, :], perm[:, :], -E, None, ALU.add))
            dve.wait_ge(selected, 2)

            def stage(place):
                b, n = place.b, place.n
                N = 4 * n
                nb = 0 if place.kind == "start" else b + 1
                for s in place.steps:
                    i = int(s[-1]) if s[-1].isdigit() else 0
                    if s[0] == "S" and s != "ST":
                        for t in range(TT):
                            bank, c = SC_AT[t]
                            w = P * (t + 1)
                            if t != 1:
                                dve.wait_ge(sc_full, 3 * N + (3 * i + max(t, 1)))
                                dve.sem_inc(apart, 1)
                            at = sc[:, bank, c:c + w]
                            dve.tensor_tensor_reduce(at, at, mask[:, S - w:S], 1.0, LOWEST, ALU.add, ALU.max,
                                                     row_max[:, t:t + 1]).then_inc(tile_max, 1)
                        dve.wait_ge(tile_max, 4 * N + (4 * i + 4))
                        dve.tensor_scalar(neg_max[:, :], row_max[:, :], -SCALE, None, ALU.mult).then_inc(max_ready, 1)
                    elif s[0] == "N":
                        dve.wait_ge(exp_done, 4 * N + (4 * i + 4))
                        dve.reciprocal(inv_sum[:, :], row_sum[:, :]).then_inc(inv_ready, 1)
                        dve.wait_ge(inv_ready, N + (i + 1))
                        for t in range(TT):
                            at = prob[:, P_OFF[t]:P_OFF[t] + P * (t + 1)]
                            dve.tensor_scalar(at, at, inv_sum[:, t:t + 1], None, ALU.mult).then_inc(prob_ready, 1)
                    elif s[:2] == "Ta":
                        r = i % 2
                        base = 18 * n + 2
                        dve.wait_ge(tp_hi, base + (4 * i + 1))
                        dve.tensor_tensor(pt_lo[:, r, 0:S], tp[:, 0, :], pt_hi[:, r, 0:S], ALU.subtract)\
                           .then_inc(tpa_free, 1)
                        dve.wait_ge(tp_hi, base + (4 * i + 3))
                        dve.tensor_tensor(pt_lo[:, r, S:896], tp[:, 1, 0:384], pt_hi[:, r, S:896], ALU.subtract)
                        dve.tensor_tensor(pt3_lo[:, r, P:2 * P], tp[:, 1, 384:S], pt3_hi[:, r, P:2 * P],
                                          ALU.subtract).then_inc(tpb_free, 1)
                    elif s[:2] == "Tb":
                        r = i % 2
                        dve.wait_ge(tp_hi, 18 * n + (2 + 4 * i + 4))
                        dve.tensor_tensor(pt_lo[:, r, 896:PT_LEN], tp[:, 0, 0:256], pt_hi[:, r, 896:PT_LEN],
                                          ALU.subtract).then_inc(tpa_free, 1)
                    elif s[:2] == "PV":
                        dve.wait_ge(at_rounded, N + (i + 1))
                        dve.tensor_tensor(at_lo[:, i, :], pv[:, :], at_hi[:, i, :], ALU.subtract).then_inc(pv_free, 1)
                    elif s[0] in "QK":
                        hi, lo = (k_hi[:, :], k_lo[:, :]) if s == "K" else (q_hi[:, i % 2, :], q_lo[:, i % 2, :])
                        dve.wait_ge(split_hi, place.split_done(s))
                        dve.tensor_tensor(lo, fb[:, place.bank(s), :], hi, ALU.subtract)\
                           .then_inc(bank_free[place.bank(s)], 1)
                    elif s == "VT":
                        base = 0 if place.kind == "start" else (18 * n + 18 if place.kind != "post" else 18 * (8 * b + 8))
                        for half, free in ((0, tpa_free), (1, tpb_free)):
                            dve.wait_ge(tp_hi, base + (half + 1))
                            dve.tensor_tensor(v_lo[:, 2 * half:2 * half + 2, :],
                                              tp[:, half, 0:256].rearrange("p (j d) -> p j d", j=2),
                                              v_hi[:, 2 * half:2 * half + 2, :], ALU.subtract).then_inc(free, 1)
                    elif s[0] == "D":
                        dve.wait_ge(job_full, place.full(s))
                        dve.tensor_tensor(hacc[:, i, :], hacc[:, i, :], fb[:, place.bank(s), :], ALU.add)\
                           .then_inc(bank_free[place.bank(s)], 1)
                    elif s == "H0":
                        dve.wait_ge(hacc_free, b + 1)
                        dve.tensor_scalar(perm_now[:, :], perm_now[:, :], E, None, ALU.add).then_inc(perm_ready, 1)
                    elif s == "G":
                        dve.tensor_copy(rows_now[:, :], rows_all[:, bass.ds(TT * nb, TT)]).then_inc(rows_ready, 1)
                        dve.tensor_copy(coef[:, :], coef_all[:, bass.ds(S * nb, S)]).then_inc(rows_ready, 1)
                    elif s[0] == "B":
                        c, half = i // 2, i % 2
                        at = h_tok[:, c, half * S:(half + 1) * S]
                        if half == 0:
                            dve.wait_ge(pos_added, 4 * nb + (c + 1))
                        dve.wait_ge(job_full, place.full(s))
                        dve.tensor_tensor(at, at, fb[:, place.bank(s), :], ALU.add)\
                           .then_inc(bank_free[place.bank(s)], 1)
                        dve.wait_ge(bank_free[place.bank(s)], place.free(s) + 1)
                        dve.bn_stats(stats[:, c, half, :], at).then_inc(h_step, 1)
                        if half == 1:
                            dve.wait_ge(h_step, 15 * nb + (3 * c + 2))
                            dve.sem_inc(apart, 1)
                            dve.bn_aggr(moments[:, c, :], stats[:, c, :, :]).then_inc(h_step, 1)
                    elif s == "L":
                        dve.wait_ge(h_step, 15 * nb + 12)
                        dve.tensor_scalar(var_eps[:, :], moments[:, :, 1], EPS, None, ALU.add).then_inc(h_step, 1)
                        dve.wait_ge(h_step, 15 * nb + 13)
                        dve.reciprocal(inv_var[:, :], var_eps[:, :]).then_inc(h_step, 1)
                        dve.wait_ge(rstd_done, nb + 1)
                        dve.scalar_tensor_tensor(out=shift[:, :], in0=moments[:, :, 0], scalar=-1.0, in1=rstd[:, :],
                                                 op0=ALU.mult, op1=ALU.mult).then_inc(h_step, 1)
                    elif s[0] == "X":
                        c, half = i // 2, i % 2
                        at = (slice(None), slice(4 * half, 4 * half + 4), slice(c * P, (c + 1) * P))
                        dve.wait_ge(split_hi, place.split_done(s))
                        dve.tensor_tensor(xn_lo[at], fb[:, place.bank(s), :].rearrange("p (j t) -> p j t", j=4),
                                          xn_hi[at], ALU.subtract).then_inc(bank_free[place.bank(s)], 1)
                    elif s == "M":
                        for j in range(KT):
                            dve.wait_ge(y_rounded, 24 * b + (j + 1))
                            dve.tensor_tensor(y_lo[:, j % 2, :], hacc[:, j, :], y_hi[:, j % 2, :], ALU.subtract)\
                               .then_inc(y_ready, 1)
                        dve.wait_ge(stat_full, 16 * b + 8)
                        dve.tensor_scalar(mean2[:, :], sc[:, 1, :], 1.0 / E, None, ALU.mult).then_inc(y_step, 1)
                        dve.wait_ge(y_step, 27 * b + 1)
                    elif s == "R":
                        for j in range(KT):
                            if j > 0:
                                dve.wait_ge(squared, 8 * b + j)
                            dve.tensor_tensor(y_raw[:, :], hacc[:, j, :], mean2[:, :], ALU.subtract)\
                               .then_inc(y_step, 1)
                            dve.wait_ge(y_rounded, 24 * b + (8 + j + 1))
                            dve.tensor_tensor(y_lo[:, j % 2, :], g_raw[:, j % 2, :], y_hi[:, j % 2, :],
                                              ALU.subtract).then_inc(y_ready, 1)
                        dve.wait_ge(stat_full, 16 * b + 16)
                        dve.tensor_scalar(rstd2[:, :], sc[:, 2, :], 1.0 / E, EPS, ALU.mult, ALU.add)\
                           .then_inc(y_step, 1)
                        dve.wait_ge(y_step, 27 * b + 10)
                        dve.reciprocal(y_raw[:, :], rstd2[:, :]).then_inc(y_step, 1)
                        dve.wait_ge(rstd2_done, b + 1)
                    elif s == "F":
                        mlp(place)

            def mlp(place):
                b = place.b
                first_job = len(place.jobs)

                def normalise(p):
                    dve.tensor_tensor(y_raw[:, :], hacc[:, p, :], mean2[:, :], ALU.subtract).then_inc(y_step, 1)
                    dve.wait_ge(y_step, 27 * b + (12 + 2 * p))
                    dve.tensor_tensor(y_raw[:, :], y_raw[:, :], rstd2[:, :], ALU.mult).then_inc(y_step, 1)

                def input_lo(p):
                    dve.wait_ge(y_rounded, 24 * b + (16 + p + 1))
                    dve.tensor_tensor(y_lo[:, p % 2, :], y_raw[:, :], y_hi[:, p % 2, :], ALU.subtract)\
                       .then_inc(y_ready, 1)

                def add_output(p):
                    dve.wait_ge(pv_full, 40 * b + (33 + p))
                    dve.tensor_tensor(hacc[:, p, :], hacc[:, p, :], pv[:, :], ALU.add).then_inc(pv_free, 1)

                def low_up(p):
                    r = p % 2
                    dve.wait_ge(wf_rounded, 16 * b + (2 * p + 2))
                    for h in range(2):
                        rows = slice(h * DH, (h + 1) * DH)
                        dve.tensor_tensor(up_lo[rows, r, h, :], wf_raw[rows, r, 0:MH], up_hi[rows, r, h, :],
                                          ALU.subtract).then_inc(up_ready, 1)

                low_up(0)
                low_up(1)
                normalise(0)
                input_lo(0)
                for hh in range(HEADS):
                    p, h = hh // 2, hh % 2
                    for kt in range(2):
                        job = first_job + 2 * hh + kt
                        dve.wait_ge(bank_free[job % 2], place.half + (job // 2 + 1))
                        dve.tensor_copy(g_hi[:, h, kt, :], g_raw[:, kt, :]).then_inc(g_rounded, 1)
                    dve.wait_ge(g_rounded, 32 * b + (2 * hh + 2))
                    dve.tensor_tensor(g_lo[:, h, 1, :], g_raw[:, 1, :], g_hi[:, h, 1, :], ALU.subtract)\
                       .then_inc(g_low_dve, 1)
                    if h == 0 and p + 1 < PAIRS:
                        normalise(p + 1)
                        input_lo(p + 1)
                    if h == 0 and p > 0:
                        add_output(p - 1)
                    if h == 0 and 1 <= p < PAIRS - 1:
                        low_up(p + 1)
                add_output(PAIRS - 1)

            walk(dve, stage)

        @block.gpsimd
        def _(pool):
            pool.sem_inc(wd_ready, 2)
            pool.sem_inc(wf_ready, 2)
            pool.sem_inc(hacc_free, 1)
            pool.wait_ge(zeroed, 3)
            pool.affine_select(out=mask[:, S - P:S], in_=mask[:, S - P:S], compare_op=ALU.is_ge, fill=LOWEST,
                               base=0, pattern=[[-1, P]], channel_multiplier=1).then_inc(selected, 1)
            pool.affine_select(out=ident[:, :], in_=ident[:, :], compare_op=ALU.not_equal, fill=1.0,
                               base=0, pattern=[[-1, P]], channel_multiplier=1).then_inc(selected, 1)

            def low_wq(place, k):
                first = {"start": 0, "post": 48}.get(place.kind, 4)
                raw, slot = (first + k) % 2, (first + k) % RQ
                pool.wait_ge(wq_rounded, place.wq + (k + 1))
                pool.tensor_tensor(wq_lo[:, slot, :], wq_raw[:, raw, :], wq_hi[:, slot, :], ALU.subtract)\
                    .then_inc(wq_ready, 1)

            def low_wd(count, m):
                pool.wait_ge(wd_rounded, count + (m + 1))
                pool.tensor_tensor(wd_lo[:, m % RD, :], wd_raw[:, m % 2, :], wd_hi[:, m % RD, :], ALU.subtract)\
                    .then_inc(wd_ready, 1)

            def low_wf(b, p):
                r = p % 2
                pool.wait_ge(wf_rounded, 16 * b + (2 * p + 2))
                for h in range(2):
                    rows = slice(h * DH, (h + 1) * DH)
                    ins = pool.tensor_tensor(dn_lo[:, r, 2 * h:2 * h + 2, rows],
                                             wf_raw[:, r, MH + h * P:MH + (h + 1) * P]
                                             .rearrange("p (k d) -> p k d", k=2),
                                             dn_hi[:, r, 2 * h:2 * h + 2, rows], ALU.subtract)
                    if h == 0:
                        pool.wait_ge(up_ready, 16 * b + (2 * p + 2))
                ins.then_inc(wf_ready, 1)

            def stage(place):
                b = place.b
                nb = 0 if place.kind == "start" else b + 1
                if place.kind == "first":
                    for m in range(RD):
                        low_wd(64 * b, m)
                for s in place.steps:
                    i = int(s[-1]) if s[-1].isdigit() else 0
                    if is_qkv(s) and not (place.kind == "last" and "X0" not in place.steps):
                        low_wq(place, place.weights[s] + RQ)
                    if s[0] == "D" and not (place.kind == "post" and i >= RD):
                        low_wd(place.wd, i + RD)
                    if s == "G":
                        pool.wait_ge(rows_ready, 2 * nb + 1)
                        if place.kind == "start":
                            pool.wait_ge(edge_step, 8)
                        else:
                            pool.wait_ge(job_full, place.full("H7"))
                            pool.sem_inc(apart, 1)
                        for c in range(TT):
                            pool.indirect_dma_start(
                                out=h_tok[:, c, :], out_offset=None, in_=table,
                                in_offset=bass.IndirectOffsetOnAxis(ap=rows_now[:, c:c + 1].bitcast(U32), axis=0))\
                                .then_inc(gathered, 16)
                    if s[0] == "A":
                        if i == 0:
                            pool.wait_ge(gathered, 64 * nb + 64)
                        pool.wait_ge(pos_in, 64 * nb + 16 * (i + 1))
                        pool.tensor_tensor(h_tok[:, i, :], h_tok[:, i, :], row_buf[:, :], ALU.add)\
                            .then_inc(pos_added, 1)
                    if s == "ST":
                        pool.wait_ge(stored, 16 * b + 16)
                        pool.sem_inc(apart, 1)
                        for k in range(KT):
                            pool.indirect_dma_start(
                                out=hacc[:, k, :], out_offset=None, in_=scratch,
                                in_offset=bass.IndirectOffsetOnAxis(ap=perm[:, k:k + 1].bitcast(U32), axis=0))\
                                .then_inc(turned, 16)
                    if s == "F":
                        mlp(b)

            def mlp(b):
                def scatter(p):
                    pool.wait_ge(pv_free, 40 * b + (34 + p))
                    pool.sem_inc(apart, 1)
                    pool.indirect_dma_start(
                        out=out, out_offset=bass.IndirectOffsetOnAxis(ap=perm_now[:, p:p + 1].bitcast(U32), axis=0),
                        in_=hacc[:, p, :], in_offset=None).then_inc(scattered, 16)

                low_wf(b, 0)
                low_wf(b, 1)
                pool.wait_ge(perm_ready, b + 1)
                for hh in range(HEADS):
                    p, h = hh // 2, hh % 2
                    pool.wait_ge(g_rounded, 32 * b + (2 * hh + 1))
                    pool.tensor_tensor(g_lo[:, h, 0, :], g_raw[:, 0, :], g_hi[:, h, 0, :], ALU.subtract)\
                        .then_inc(g_low_pool, 1)
                    if h == 0 and 1 <= p < PAIRS - 1:
                        low_wf(b, p + 1)
                    if h == 1 and p > 0:
                        scatter(p - 1)
                scatter(PAIRS - 1)
                pool.wait_ge(scattered, 128 * b + 128)
                pool.sem_inc(hacc_free, 1)

            start = Place([], 0, 0, "start")
            for m in range(RQ):
                low_wq(start, m)
            walk(pool, stage)


def kernel(x, L0_tok_kernel, L0_tok_bias, L0_tok_pos_emb, L0_attn_w_qkv, L0_attn_w_dense,
           L0_ffn_up, L0_ffn_down, L0_ffn_perm):
    import numpy as np
    import concourse.bacc as bacc
    from concourse.bass_utils import run_bass_kernel_spmd

    x = np.asarray(x)
    x_cols = x.reshape(B * TT, P).T
    x_row = x.reshape(1, B * S)
    table = np.asarray(L0_tok_kernel).reshape(VOCAB, E)

    edge_cols = np.zeros((32, 3), np.float32)
    edge_cols[:, 1], edge_cols[:, 2] = 1, 1
    n = SHARDS - 1
    for s in range(n):
        edge_cols[s, 0:2] = 1, (s + 1) * VS
        edge_cols[n + s, 0:2] = -1, 1 - (s + 1) * VS
    edge_cols[2 * n] = 0, 0, SHARDS

    w = np.asarray(L0_attn_w_qkv).reshape(G * (HQ + 2), D, KT, P).transpose(0, 3, 2, 1).reshape(-1, P, E)
    order = []
    for g in range(G):
        q, k, v = g * HQ, G * HQ + g, G * HQ + G + g
        order += [q, k, q + 1, v, q + 2, q + 3]
    w_qkv = w[order + order[:RQ]]
    w_dense = np.asarray(L0_attn_w_dense).reshape(KT, P, G, HQ, D).transpose(2, 0, 4, 3, 1)\
        .reshape(G * KT, P, HQ * P)
    up = np.asarray(L0_ffn_up).reshape(PAIRS, P, MH)
    down = np.asarray(L0_ffn_down).reshape(PAIRS, 2, 2, P, DH).transpose(0, 3, 1, 2, 4).reshape(PAIRS, P, MH)
    w_mlp = np.concatenate([up, down], axis=2)
    perm_cols = np.asarray(L0_ffn_perm).reshape(KT, P).T

    arrays = {
        "x_cols": x_cols, "x_row": x_row, "table": table,
        "bias": np.asarray(L0_tok_bias).reshape(1, E), "pos": np.asarray(L0_tok_pos_emb),
        "edge_cols": edge_cols, "w_qkv": w_qkv, "w_dense": w_dense, "w_mlp": w_mlp, "perm_cols": perm_cols,
    }
    arrays = {name: np.ascontiguousarray(a) for name, a in arrays.items()}
    nc = bacc.Bacc("TRN2", target_bir_lowering=False, num_devices=1)
    args = [nc.dram_tensor(f"in_{name}", a.shape, mybir.dt.from_np(a.dtype), kind="ExternalInput").ap()
            for name, a in arrays.items()]
    out = nc.dram_tensor("out_rows", [B * E, S], F32, kind="ExternalOutput").ap()
    tower_kernel(nc, *args, out)
    r = run_bass_kernel_spmd(nc, [{f"in_{name}": a for name, a in arrays.items()}], core_ids=[0])
    rows = r.results[0]["out_rows"]
    return rows.reshape(B, E, S).transpose(0, 2, 1)
```

```python
from contextlib import ExitStack

import concourse.bass as bass
from concourse import mybir

F32 = mybir.dt.float32
F32R = mybir.dt.float32r
BF16 = mybir.dt.bfloat16
I32 = mybir.dt.int32
U32 = mybir.dt.uint32
ALU = mybir.AluOpType
ACT = mybir.ActivationFunctionType

P = 128
B, S, E = 4, 512, 1024
G, HQ, D = 8, 4, 128
KT = E // P
TT = S // P
SHARDS, VS = 8, 1575
VOCAB = SHARDS * VS
HEADS, DH, MH = 16, 64, 256
UNITS = HEADS * MH // P
PAIRS = HEADS // 2
EDGE = 2 * (SHARDS - 1) + 1
SCALE = float(D) ** -0.5
EPS = 1e-5
LOWEST = -3.0e38

RQ, RD, RF = 3, 4, 2
QKV_TILES = G * (HQ + 2)

P_OFF = [0, 128, 384, 768]
P_LEN = 1280
SC_AT = [(0, 0), (0, 256), (1, 0), (2, 0)]
PT_OFF = [0, 512, 896]
PT_LEN = 1152

MID = ("S0 N0 Q2 D0 Ta0 D1 Tb0 S1 N1 Q3 D2 Ta1 D3 Tb1 S2 D4 D5 N2 D6 D7 PV0 "
       "Ta2 Q0 Tb2 S3 PV1 K N3 Q1 Ta3 PV2 Tb3 V PV3 VT").split()
FIRST = ("S0 N0 Q2 H0 Ta0 H1 Tb0 S1 N1 Q3 H2 Ta1 H3 Tb1 S2 H4 H5 N2 H6 H7 G PV0 "
         "Ta2 Q0 Tb2 S3 PV1 K A0 N3 Q1 A1 Ta3 PV2 Tb3 A2 V A3 PV3 VT").split()
LAST = ("S0 N0 Q2 D0 Ta0 B0 B1 D1 Tb0 S1 N1 Q3 D2 Ta1 B2 B3 D3 Tb1 S2 D4 D5 N2 D6 D7 PV0 Ta2 B4 B5 "
        "Tb2 S3 PV1 N3 Ta3 B6 B7 La PV2 Tb3 Lb PV3").split()
LAST_ALONE = [s for s in LAST if s[0] not in "BL"]
POST = ("D0 X0 X1 D1 X2 X3 D2 M0 X4 X5 D3 M1 X6 X7 D4 M2 D5 M3 D6 M4 D7 M5 Q0 M6 M7 K R0 R1 Q1 R2 R3 R4 "
        "V R5 R6 R7 VT F").split()
POST_ALONE = [s for s in POST if s[0] in "DMRF"]
START = "G A0 B0 B1 A1 B2 B3 A2 B4 B5 A3 B6 B7 La Lb X0 X1 X2 X3 X4 X5 X6 X7 Q0 K Q1 V VT".split()


def is_job(s):
    return s[0] in "QKDH" or s == "V"


def number(steps, which):
    out, n = {}, 0
    for s in steps:
        if which(s):
            out[s] = n
            n += 1
    return out


def is_qkv(s):
    return s[0] in "QK" or s == "V"


def is_split_job(s):
    return s[0] in "QK"


class Place:

    def __init__(self, steps, b, g, kind):
        self.b, self.g, self.steps, self.kind = b, g, steps, kind
        self.n = 8 * b + g
        if kind == "start":
            self.half, self.split, self.wq = 0, 0, 0
        elif kind == "post":
            self.half, self.split, self.wq = 56 + 76 * b, 3 + 40 * b + 37, 4 + 48 * b + 44
        else:
            self.half, self.split, self.wq = 2 + 76 * b + 7 * g, 3 + 40 * b + 5 * g, 4 + 48 * b + 6 * g
        self.wd = 64 * b + 56 if kind == "post" else 64 * b + 8 * (g - 1)
        self.wq_tile = 0 if kind in ("start", "post") else 4 + 6 * g
        self.wd_tile = 56 if kind == "post" else 8 * (g - 1)
        self.jobs = number(steps, is_job)
        self.splits = number(steps, is_split_job)
        self.weights = number(steps, is_qkv)

    def bank(self, s):
        return self.jobs[s] % 2

    def full(self, s):
        return 2 * self.half + (self.jobs[s] + 1)

    def free(self, s):
        return self.half + self.jobs[s] // 2

    def split_done(self, s):
        return self.split + (self.splits[s] + 1)

    def wq_at(self, s):
        return self.wq + self.weights[s]

    def wq_slot(self, s, n, ahead=0):
        first = {"start": 0, "post": 48}.get(self.kind, 4)
        return (first + self.weights[s] + ahead) % n


def tower_kernel(nc, x_cols, x_row, table, bias, pos, edge_cols, w_qkv, w_dense, w_up, w_down, perm_cols, out):
    scratch = nc.dram_tensor("h1_rows", [E, S], F32).ap()
    ctx = ExitStack()
    with ctx:
        def sb(name, shape, dt, at=ctx):
            return at.enter_context(nc.sbuf_tensor(name, shape, dt))

        def ps(name, shape, dt=F32):
            return ctx.enter_context(nc.psum_tensor(name, shape, dt))

        def sem(name):
            return ctx.enter_context(nc.semaphore(name))

        xn_hi = sb("xn_hi", [P, KT, S], F32R)
        xn_lo = sb("xn_lo", [P, KT, S], F32R)
        h_tok = sb("h_tok", [P, TT, E], F32)
        row_buf = sb("row_buf", [P, E], F32)
        hacc = sb("hacc", [P, KT, S], F32)
        wq_raw = sb("wq_raw", [P, 2, E], F32)
        wq_hi = sb("wq_hi", [P, RQ, E], F32R)
        wq_lo = sb("wq_lo", [P, RQ, E], F32R)
        wd_raw = sb("wd_raw", [P, 2, HQ * P], F32)
        wd_hi = sb("wd_hi", [P, RD, HQ * P], F32R)
        wd_lo = sb("wd_lo", [P, RD, HQ * P], F32R)
        q_hi = sb("q_hi", [P, 2, S], F32R)
        q_lo = sb("q_lo", [P, 2, S], F32R)
        k_hi = sb("k_hi", [P, S], F32R)
        k_lo = sb("k_lo", [P, S], F32R)
        v_hi = sb("v_hi", [P, TT, D], F32R)
        v_lo = sb("v_lo", [P, TT, D], F32R)
        v_feat = sb("v_feat", [P, S], F32)
        pt3_hi = sb("pt3_hi", [P, 2, 256], F32R)
        pt3_lo = sb("pt3_lo", [P, 2, 256], F32R)
        mask = sb("mask", [P, S], F32)
        ident = sb("ident", [P, P], F32)
        ones = sb("ones", [P, P], F32R)
        edges = sb("edges", [96, E], BF16)
        coef = sb("coef", [96, S], BF16)
        coef_all = sb("coef_all", [96, B * S], BF16)
        edge_consts = sb("edge_consts", [96, 3], F32)
        xi = sb("xi", [P, B * TT], I32)
        rows_all = sb("rows_all", [P, B * TT], I32)
        rows_now = sb("rows_now", [P, TT], I32)
        perm = sb("perm", [P, KT], I32)
        perm_now = sb("perm_now", [P, KT], I32)
        stats = sb("stats", [P, TT, 2, 6], F32)
        moments = sb("moments", [P, TT, 2], F32)
        var_eps = sb("var_eps", [P, TT], F32)
        inv_var = sb("inv_var", [P, TT], F32)
        rstd = sb("rstd", [P, TT], F32)
        shift = sb("shift", [P, TT], F32)
        row_max = sb("row_max", [P, TT], F32)
        neg_max = sb("neg_max", [P, TT], F32)
        row_sum = sb("row_sum", [P, TT], F32)
        inv_sum = sb("inv_sum", [P, TT], F32)
        up_hi = sb("up_hi", [P, RF, 2 * MH], F32R)
        up_lo = sb("up_lo", [P, RF, 2 * MH], F32R)
        dn_hi = sb("dn_hi", [P, RF, 4 * P], F32R)
        dn_lo = sb("dn_lo", [P, RF, 4 * P], F32R)

        with ExitStack() as own:
            at_hi = sb("at_hi", [P, HQ, S], F32R, own)
            at_lo = sb("at_lo", [P, HQ, S], F32R, own)
            pt_hi = sb("pt_hi", [P, 2, PT_LEN], F32R, own)
            pt_lo = sb("pt_lo", [P, 2, PT_LEN], F32R, own)
            prob = sb("prob", [P, P_LEN], F32, own)
        with ExitStack() as own:
            g_hi = sb("g_hi", [P, 2, 2, S], F32R, own)
            g_lo = sb("g_lo", [P, 2, 2, S], F32R, own)
            y_hi = sb("y_hi", [P, 2, S], F32R, own)
            y_lo = sb("y_lo", [P, 2, S], F32R, own)
            y_raw = sb("y_raw", [P, S], F32, own)
            mean2 = sb("mean2", [P, S], F32, own)
            rstd2 = sb("rstd2", [P, S], F32, own)
            g_raw = sb("g_raw", [P, 2, S], F32, own)
            up_raw = sb("up_raw", [P, 2 * MH], F32, own)
            dn_raw = sb("dn_raw", [P, HQ * P], F32, own)

        sc = ps("sc", [P, 3, S])
        tp = ps("tp", [P, 2, S])
        pv = ps("pv", [P, S])
        fb = ps("fb", [P, 2, S])

        const_in = sem("const_in")
        edge_in = sem("edge_in")
        edge_step = sem("edge_step")
        zeroed = sem("zeroed")
        selected = sem("selected")
        rows_ready = sem("rows_ready")
        gathered = sem("gathered")
        pos_in = sem("pos_in")
        pos_added = sem("pos_added")
        h_step = sem("h_step")
        rstd_done = sem("rstd_done")
        row_ready = sem("row_ready")
        job_full = sem("job_full")
        bank_free = [sem("bank0_free"), sem("bank1_free")]
        split_hi = sem("split_hi")
        wq_in = [sem("wq_in0"), sem("wq_in1")]
        wq_rounded = sem("wq_rounded")
        wq_ready = sem("wq_ready")
        wd_in = [sem("wd_in0"), sem("wd_in1")]
        wd_rounded = sem("wd_rounded")
        wd_ready = sem("wd_ready")
        up_in = sem("up_in")
        up_rounded = sem("up_rounded")
        up_ready = sem("up_ready")
        dn_in = sem("dn_in")
        dn_rounded = sem("dn_rounded")
        dn_ready = sem("dn_ready")
        b_full = sem("b_full")
        b_free = sem("b_free")
        x_full = sem("x_full")
        x_hi = sem("x_hi")
        x_free = sem("x_free")
        tp_full = sem("tp_full")
        tp_hi = sem("tp_hi")
        tpa_free = sem("tpa_free")
        tpb_free = sem("tpb_free")
        sc_full = sem("sc_full")
        tile_max = sem("tile_max")
        max_ready = sem("max_ready")
        exp_done = sem("exp_done")
        inv_ready = sem("inv_ready")
        prob_ready = sem("prob_ready")
        pv_full = sem("pv_full")
        at_rounded = sem("at_rounded")
        pv_free = sem("pv_free")
        stored = sem("stored")
        turned = [sem(f"turned{k}") for k in range(KT)]
        y_rounded = sem("y_rounded")
        y_ready = sem("y_ready")
        y_step = sem("y_step")
        squared = sem("squared")
        stat_full = sem("stat_full")
        rstd2_done = sem("rstd2_done")
        perm_ready = sem("perm_ready")
        g_rounded = sem("g_rounded")
        g_low_pool = sem("g_low_pool")
        g_low_dve = sem("g_low_dve")
        scattered = sem("scattered")
        hacc_free = sem("hacc_free")
        apart = sem("apart")

        def gelu_out(w):
            return g_raw[:, w, :] if w < 2 else row_buf[:, (w - 2) * S:(w - 1) * S]

        block = ctx.enter_context(nc.Block())

        def walk(eng, stage):
            stage(Place(START, 0, 0, "start"))

            def batch(b, last):
                stage(Place(FIRST if not last else [s for s in FIRST if s[0] not in "GA"], b, 0, "first"))
                with eng.Fori(1, G - 1) as g:
                    stage(Place(MID, b, g, "mid"))
                stage(Place(LAST_ALONE if last else LAST, b, G - 1, "last"))
                stage(Place(POST_ALONE if last else POST, b, 0, "post"))

            with eng.Fori(0, B - 1) as b:
                batch(b, False)
            batch(B - 1, True)

        @block.sync
        def _(sp):
            sp.dma_start(xi[:, :], x_cols).then_inc(const_in, 16)
            sp.dma_start(perm[:, :], perm_cols).then_inc(const_in, 16)
            for part in range(3):
                at = slice(32 * part, 32 * part + 32)
                sp.dma_start(edge_consts[at, :], edge_cols).then_inc(const_in, 16)
                sp.dma_start(h_tok[at, 0:2, :].rearrange("p a n -> p (a n)").bitcast(I32),
                             x_row.partition_broadcast(32)).then_inc(const_in, 16)
            sp.wait_ge(zeroed, 1)
            shards = table.rearrange("(s v) e -> s v e", v=VS)
            for part in range(3):
                at = 32 * part
                n = SHARDS - 1
                sp.dma_start(row_buf[at:at + n, :], shards[0:n, VS - 1, :]).then_inc(edge_in, 16)
                sp.dma_start(row_buf[at + n:at + 2 * n, :], shards[1:SHARDS, 0, :]).then_inc(edge_in, 16)
                sp.dma_start(row_buf[at + 2 * n:at + EDGE, :], bias).then_inc(edge_in, 16)

            def load_wq(slot, index):
                sp.dma_start(wq_raw[:, slot, :], w_qkv[index]).then_inc(wq_in[slot], 16)

            for m in range(RQ):
                if m >= 2:
                    sp.wait_ge(wq_ready, m - 1)
                load_wq(m % 2, m)

            def load_wd(place, m):
                sp.wait_ge(wd_ready, place.wd + (m + 1))
                sp.dma_start(wd_raw[:, m % 2, :], w_dense[place.wd_tile + m]).then_inc(wd_in[m % 2], 16)

            def stage(place):
                b = place.b
                if place.kind == "first":
                    for m in range(RD):
                        sp.wait_ge(wd_ready, 64 * b + (m + 1))
                        sp.dma_start(wd_raw[:, m % 2, :], w_dense[m]).then_inc(wd_in[m % 2], 16)
                for s in place.steps:
                    if is_qkv(s):
                        if "B0" not in place.steps and place.kind == "last":
                            continue
                        k = place.weights[s] + RQ
                        sp.wait_ge(wq_ready, place.wq + (k - 1))
                        load_wq(place.wq_slot(s, 2, RQ), place.wq_tile + k)
                    if s[0] == "D" and not (place.kind == "post" and int(s[1]) >= RD):
                        load_wd(place, int(s[1]) + RD)
                    if s[0] == "A":
                        c = int(s[1])
                        done = 4 * (b + 1) if place.kind != "start" else 0
                        if c > 0:
                            sp.wait_ge(pos_added, done + c)
                        elif place.kind == "start":
                            sp.wait_ge(edge_step, 7)
                        else:
                            sp.wait_ge(job_full, place.full("H0"))
                        sp.dma_start(row_buf[:, :], pos[c * P:(c + 1) * P, :]).then_inc(pos_in, 16)
                    if s[0] == "D" and place.kind == "post":
                        sp.wait_ge(bank_free[place.bank(s)], place.free(s) + 1)
                        m = int(s[1])
                        sp.dma_start(scratch[m * P:(m + 1) * P, :], hacc[:, m, :]).then_inc(stored, 16)
                    if s == "F":
                        for p in range(PAIRS):
                            sp.wait_ge(up_ready, 8 * b + (p + 1))
                            sp.dma_start(up_raw[:, :], w_up[p]).then_inc(up_in, 16)
                            sp.wait_ge(dn_ready, 8 * b + (p + 1))
                            sp.dma_start(dn_raw[:, :], w_down[p]).then_inc(dn_in, 16)

            walk(sp, stage)

        @block.tensor
        def _(pe):
            def product(dst, a_hi, a_lo, b_hi, b_lo, first, last):
                pe.matmul(dst, a_hi, b_hi, start=first, stop=False)
                pe.matmul(dst, a_hi, b_lo, start=False, stop=False)
                return pe.matmul(dst, a_lo, b_hi, start=False, stop=last)

            def scores(place, i):
                n, q = place.n, i % 2
                if i == 0:
                    pe.wait_ge(bank_free[0], place.half - 1)
                    pe.wait_ge(bank_free[1], place.half - 1)
                if i == 1:
                    pe.wait_ge(bank_free[0], place.half)
                if i == 2:
                    pe.wait_ge(bank_free[place.bank("Q2")], place.free("Q2") + 1)
                if i == 3:
                    pe.wait_ge(bank_free[place.bank("Q3")], place.free("Q3") + 1)
                if place.kind == "last" and "B0" in place.steps and i > 0:
                    pe.wait_ge(b_free, 8 * (place.b + 1) + (2 * i + 1))
                for t in range(TT):
                    bank, c = SC_AT[t]
                    w = max(256, P * (t + 1))
                    qt = slice(t * P, (t + 1) * P)
                    mm = product(sc[:, bank, c:c + w], q_hi[:, q, qt], q_lo[:, q, qt],
                                 k_hi[:, 0:w], k_lo[:, 0:w], True, True)
                    if t > 0:
                        mm.then_inc(sc_full, 1)

            def turn(place, i, part):
                def block_(bank, c, t, j):
                    return pe.transpose(tp[:, bank, c:c + P], prob[:, P_OFF[t] + j * P:P_OFF[t] + (j + 1) * P],
                                        ident[:, :])
                n = place.n
                if part == "a":
                    pe.wait_ge(prob_ready, 16 * n + (4 * i + 4))
                    pe.wait_ge(tpa_free, 9 * n + (2 * i + 1))
                    for t in range(TT):
                        last = block_(0, t * P, t, 0)
                    last.then_inc(tp_full, 1)
                    pe.wait_ge(tpb_free, 5 * n + (i + 1))
                    for t in range(1, TT):
                        block_(1, (t - 1) * P, t, 1)
                    block_(1, 3 * P, 3, 3).then_inc(tp_full, 1)
                else:
                    pe.wait_ge(tpa_free, 9 * n + (2 * i + 2))
                    block_(0, 0, 2, 2)
                    block_(0, P, 3, 2).then_inc(tp_full, 1)

            def values(place, i):
                n, r = place.n, i % 2
                pe.wait_ge(tpa_free, 9 * n + (2 * i + 3))
                pe.wait_ge(pv_free, 40 * place.b + 4 * place.g + (i + 1))
                for j in range(TT):
                    if j < 3:
                        cols = slice(j * P, S)
                        at = slice(PT_OFF[j], PT_OFF[j] + S - j * P)
                        b_hi, b_lo = pt_hi[:, r, at], pt_lo[:, r, at]
                    else:
                        cols = slice(S - 256, S)
                        b_hi, b_lo = pt3_hi[:, r, :], pt3_lo[:, r, :]
                    mm = product(pv[:, cols], v_hi[:, j, :], v_lo[:, j, :], b_hi, b_lo, j == 0, j == 3)
                mm.then_inc(pv_full, 1)

            def start_job(place, s):
                if not (place.kind == "start" and place.jobs[s] < 2):
                    pe.wait_ge(bank_free[place.bank(s)], place.free(s))
                return fb[:, place.bank(s), :]

            def project(place, s):
                slot = place.wq_slot(s, RQ)
                pe.wait_ge(wq_ready, place.wq_at(s) + 1)
                dst = start_job(place, s)
                for k in range(KT):
                    w = slice(k * P, (k + 1) * P)
                    mm = product(dst, wq_hi[:, slot, w], wq_lo[:, slot, w], xn_hi[:, k, :], xn_lo[:, k, :],
                                 k == 0, k == KT - 1)
                mm.then_inc(job_full, 1)

            def dense(place, s):
                m = int(s[1])
                if m == 0:
                    pe.wait_ge(pv_free, 40 * place.b + (33 if place.kind == "post" else 4 * place.g + 1))
                pe.wait_ge(wd_ready, place.wd + (m + 3))
                dst = start_job(place, s)
                for h in range(HQ):
                    w = slice(h * P, (h + 1) * P)
                    mm = product(dst, wd_hi[:, m % RD, w], wd_lo[:, m % RD, w], at_hi[:, h, :], at_lo[:, h, :],
                                 h == 0, h == HQ - 1)
                mm.then_inc(job_full, 1)

            def stage(place):
                b = place.b
                for s in place.steps:
                    k = int(s[-1]) if s[-1].isdigit() else 0
                    if s[0] == "S" and s != "ST":
                        scores(place, k)
                    elif s[:2] in ("Ta", "Tb"):
                        turn(place, k, s[1])
                    elif s[:2] == "PV":
                        values(place, k)
                    elif is_qkv(s):
                        if s == "Q0" and place.kind in ("start", "post"):
                            pe.wait_ge(x_free, 8 if place.kind == "start" else 8 * b + 16)
                        project(place, s)
                    elif s[0] == "D":
                        dense(place, s)
                    elif s[0] == "H":
                        c, half = k // 2, k % 2
                        dst = start_job(place, s)
                        for j in range(4):
                            f = (4 * half + j) * P
                            mm = pe.transpose(dst[:, j * P:(j + 1) * P], h_tok[:, c, f:f + P], ident[:, :])
                        mm.then_inc(job_full, 1)
                    elif s[0] == "B":
                        c, half = k // 2, k % 2
                        nb = 0 if place.kind == "start" else b + 1
                        if k == 0:
                            pe.wait_ge(rows_ready, 2 * nb + 2)
                            pe.wait_ge(edge_step, 10)
                        pe.wait_ge(b_free, 8 * nb + max(k, 1))
                        pe.matmul(sc[:, 1 + half, :], coef[:, c * P:(c + 1) * P], edges[:, half * S:(half + 1) * S],
                                  start=True, stop=True).then_inc(b_full, 1)
                    elif s[0] == "X":
                        c, half = k // 2, k % 2
                        nb = 0 if place.kind == "start" else b + 1
                        if k == 0 and place.kind == "post":
                            pe.wait_ge(tpa_free, 72 * b + 72)
                            pe.wait_ge(tpb_free, 40 * b + 40)
                        if half == 0:
                            pe.wait_ge(row_ready, 4 * nb + (c + 1))
                        if k >= 2:
                            pe.wait_ge(x_free, 8 * nb + (k - 1))
                        for j in range(4):
                            f = (4 * half + j) * P
                            mm = pe.transpose(tp[:, half, j * P:(j + 1) * P], row_buf[:, f:f + P], ident[:, :])
                        mm.then_inc(x_full, 1)
                    elif s == "VT":
                        n = 0 if place.kind == "start" else (place.n + 1 if place.kind != "post" else 8 * b + 8)
                        pe.wait_ge(bank_free[place.bank("V")], place.free("V") + 1)
                        if place.kind not in ("start", "post"):
                            pe.wait_ge(tpa_free, 9 * n)
                            pe.wait_ge(tpb_free, 5 * n)
                        for j in range(TT):
                            mm = pe.transpose(tp[:, j // 2, (j % 2) * P:(j % 2 + 1) * P],
                                              v_feat[:, j * P:(j + 1) * P], ident[:, :])
                            if j % 2:
                                mm.then_inc(tp_full, 1)
                    elif s[0] in "MR":
                        bank, done = (1, 0) if s[0] == "M" else (2, 8)
                        pe.wait_ge(y_ready, 24 * b + (done + k + 1))
                        pe.matmul(sc[:, bank, :], ones[:, :], y_hi[:, k % 2, :], start=k == 0, stop=False)
                        pe.matmul(sc[:, bank, :], ones[:, :], y_lo[:, k % 2, :], start=False, stop=k == KT - 1)\
                            .then_inc(stat_full, 1)
                    elif s == "F":
                        mlp(place)

            def mlp(place):
                b = place.b
                first_job = len(place.jobs)
                for u in range(UNITS + 3):
                    if u < UNITS:
                        p, w = u // 4, u % 4
                        if w == 0:
                            pe.wait_ge(up_ready, 8 * b + (p + 2))
                            pe.wait_ge(y_ready, 24 * b + (16 + p + 1))
                        job = first_job + u
                        pe.wait_ge(bank_free[job % 2], place.half + job // 2)
                        cols = slice(w * P, (w + 1) * P)
                        product(fb[:, job % 2, :], up_hi[:, p % 2, cols], up_lo[:, p % 2, cols],
                                y_hi[:, p % 2, :], y_lo[:, p % 2, :], True, True).then_inc(job_full, 1)
                    if u >= 3:
                        p, w = (u - 3) // 4, (u - 3) % 4
                        if w == 0:
                            pe.wait_ge(g_low_pool, 8 * b + (p + 1))
                            pe.wait_ge(dn_ready, 8 * b + (p + 2))
                            pe.wait_ge(pv_free, 40 * b + (33 + p))
                        else:
                            pe.wait_ge(g_low_dve, 24 * b + (3 * p + w))
                        cols = slice(w * P, (w + 1) * P)
                        mm = product(pv[:, :], dn_hi[:, p % 2, cols], dn_lo[:, p % 2, cols],
                                     g_hi[:, w // 2, w % 2, :], g_lo[:, w // 2, w % 2, :], w == 0, w == 3)
                        if w == 3:
                            mm.then_inc(pv_full, 1)

            pe.wait_ge(zeroed, 4)
            pe.wait_ge(selected, 2)
            walk(pe, stage)

        @block.scalar
        def _(act):
            copy = ACT.Copy

            def split_wq(place, k):
                first = {"start": 0, "post": 48}.get(place.kind, 4)
                raw, slot = (first + k) % 2, (first + k) % RQ
                act.wait_ge(wq_in[raw], 16 * half_up(place, k))
                act.activation(wq_hi[:, slot, :], wq_raw[:, raw, :], copy).then_inc(wq_rounded, 1)

            def half_up(place, k):
                base = {"start": 0, "post": 24 + 24 * place.b}.get(place.kind, 2 + 24 * place.b + 3 * place.g)
                return base + (k // 2 + 1)

            def split_wd(place, m):
                base = 32 * place.b + (28 if place.kind == "post" else 4 * (place.g - 1))
                act.wait_ge(wd_in[m % 2], 16 * (base + (m // 2 + 1)))
                act.activation(wd_hi[:, m % RD, :], wd_raw[:, m % 2, :], copy).then_inc(wd_rounded, 1)

            def split_up(b, p):
                act.wait_ge(up_in, 16 * (8 * b + (p + 1)))
                act.activation(up_hi[:, p % 2, :], up_raw[:, :], copy).then_inc(up_rounded, 1)

            def split_down(b, p):
                act.wait_ge(dn_in, 16 * (8 * b + (p + 1)))
                act.activation(dn_hi[:, p % 2, :], dn_raw[:, :], copy).then_inc(dn_rounded, 1)

            def stage(place):
                b, n = place.b, place.n
                if place.kind == "first":
                    for m in range(RD):
                        act.wait_ge(wd_in[m % 2], 16 * (32 * b + (m // 2 + 1)))
                        act.activation(wd_hi[:, m % RD, :], wd_raw[:, m % 2, :], copy).then_inc(wd_rounded, 1)
                for s in place.steps:
                    i = int(s[-1]) if s[-1].isdigit() else 0
                    if s[0] == "S" and s != "ST":
                        act.wait_ge(max_ready, 4 * n + (i + 1))
                        for t in range(TT):
                            bank, c = SC_AT[t]
                            w = P * (t + 1)
                            act.activation(prob[:, P_OFF[t]:P_OFF[t] + w], sc[:, bank, c:c + w], ACT.Exp,
                                           bias=neg_max[:, t:t + 1], scale=SCALE,
                                           accum_out=row_sum[:, t:t + 1]).then_inc(exp_done, 1)
                    elif s[:2] == "Ta":
                        r = i % 2
                        act.wait_ge(tp_full, 14 * n + (3 * i + 3))
                        act.activation(pt_hi[:, r, 0:S], tp[:, 0, :], copy).then_inc(tp_hi, 1)
                        act.wait_ge(tp_full, 14 * n + (3 * i + 4))
                        act.activation(pt_hi[:, r, S:S + 384], tp[:, 1, 0:384], copy).then_inc(tp_hi, 1)
                        act.activation(pt3_hi[:, r, P:2 * P], tp[:, 1, 384:S], copy).then_inc(tp_hi, 1)
                    elif s[:2] == "Tb":
                        act.wait_ge(tp_full, 14 * n + (3 * i + 5))
                        act.activation(pt_hi[:, i % 2, 896:PT_LEN], tp[:, 0, 0:256], copy).then_inc(tp_hi, 1)
                    elif s[:2] == "PV":
                        act.wait_ge(pv_full, 40 * b + 4 * place.g + (i + 1))
                        act.activation(at_hi[:, i, :], pv[:, :], copy).then_inc(at_rounded, 1)
                    elif s[0] in "QK":
                        act.wait_ge(job_full, place.full(s))
                        dst = k_hi[:, :] if s == "K" else q_hi[:, i % 2, :]
                        act.activation(dst, fb[:, place.bank(s), :], copy).then_inc(split_hi, 1)
                    elif s == "V":
                        act.wait_ge(job_full, place.full(s))
                        act.activation(v_feat[:, :], fb[:, place.bank(s), :], copy)\
                           .then_inc(bank_free[place.bank(s)], 1)
                    elif s == "VT":
                        base = 0 if place.kind == "start" else (14 * n + 14 if place.kind != "post" else 14 * (8 * b + 8))
                        for half in range(2):
                            act.wait_ge(tp_full, base + (half + 1))
                            act.activation(v_hi[:, 2 * half:2 * half + 2, :],
                                           tp[:, half, 0:256].rearrange("p (j d) -> p j d", j=2), copy)\
                               .then_inc(tp_hi, 1)
                    elif s[0] == "H":
                        c, half = i // 2, i % 2
                        if i == 0:
                            act.wait_ge(hacc_free, b + 1)
                        act.wait_ge(job_full, place.full(s))
                        act.activation(hacc[:, 4 * half:4 * half + 4, c * P:(c + 1) * P],
                                       fb[:, place.bank(s), :].rearrange("p (j t) -> p j t", j=4), copy)\
                           .then_inc(bank_free[place.bank(s)], 1)
                    elif s == "La":
                        nb = 0 if place.kind == "start" else b + 1
                        act.wait_ge(h_step, 15 * nb + 14)
                        act.activation(rstd[:, :], inv_var[:, :], ACT.Sqrt).then_inc(rstd_done, 1)
                    elif s[0] == "X":
                        c, half = i // 2, i % 2
                        nb = 0 if place.kind == "start" else b + 1
                        if half == 0:
                            if c == 0:
                                act.wait_ge(h_step, 15 * nb + 15)
                            else:
                                act.wait_ge(x_full, 8 * nb + i)
                            act.activation(row_buf[:, :], h_tok[:, c, :], ACT.Identity,
                                           scale=rstd[:, c:c + 1], bias=shift[:, c:c + 1]).then_inc(row_ready, 1)
                        act.wait_ge(x_full, 8 * nb + (i + 1))
                        act.activation(xn_hi[:, 4 * half:4 * half + 4, c * P:(c + 1) * P],
                                       tp[:, half, :].rearrange("p (j t) -> p j t", j=4), copy).then_inc(x_hi, 1)
                    elif s[0] == "M":
                        act.wait_ge(bank_free[place.bank(f"D{i}")], place.free(f"D{i}") + 1)
                        if i >= 2:
                            act.wait_ge(stat_full, 16 * b + (i - 1))
                        act.activation(y_hi[:, i % 2, :], hacc[:, i, :], copy).then_inc(y_rounded, 1)
                    elif s[0] == "R":
                        centred = rstd2 if i % 2 else y_raw
                        act.wait_ge(y_step, 27 * b + (i + 2))
                        act.wait_ge(stat_full, 16 * b + (8 + i - 1))
                        act.activation(g_raw[:, i % 2, :], centred[:, :], ACT.Square).then_inc(squared, 1)
                        act.wait_ge(squared, 8 * b + (i + 1))
                        act.activation(y_hi[:, i % 2, :], g_raw[:, i % 2, :], copy).then_inc(y_rounded, 1)
                    elif s == "F":
                        mlp(place)
                    if is_qkv(s) and not (place.kind == "last" and "B0" not in place.steps):
                        split_wq(place, place.weights[s] + RQ)
                    if s[0] == "D" and not (place.kind == "post" and i >= RD):
                        act.wait_ge(job_full, place.full(s))
                        split_wd(place, i + RD)

            def mlp(place):
                b = place.b
                first_job = len(place.jobs)
                split_up(b, 0)
                split_down(b, 0)
                act.wait_ge(y_step, 27 * b + 11)
                act.activation(rstd2[:, :], y_raw[:, :], ACT.Sqrt).then_inc(rstd2_done, 1)

                def input_hi(p):
                    act.wait_ge(y_step, 27 * b + (13 + 2 * p))
                    act.activation(y_hi[:, p % 2, :], y_raw[:, :], copy).then_inc(y_rounded, 1)

                input_hi(0)
                for u in range(UNITS):
                    p, w = u // 4, u % 4
                    job = first_job + u
                    act.wait_ge(job_full, 2 * place.half + (job + 1))
                    if u >= 4:
                        if w == 0:
                            act.wait_ge(g_low_pool, 8 * b + p)
                        else:
                            act.wait_ge(g_low_dve, 24 * b + (3 * (p - 1) + w))
                    act.activation(gelu_out(w), fb[:, job % 2, :], ACT.Gelu).then_inc(bank_free[job % 2], 1)
                    if w == 0 and p + 1 < PAIRS:
                        split_up(b, p + 1)
                    if w == 1 and p + 1 < PAIRS:
                        input_hi(p + 1)
                    if w == 3 and p + 1 < PAIRS:
                        if p >= 1:
                            act.wait_ge(pv_full, 40 * b + (32 + p))
                        split_down(b, p + 1)

            for m in range(RQ):
                act.wait_ge(wq_in[m % 2], 16 * (m // 2 + 1))
                act.activation(wq_hi[:, m, :], wq_raw[:, m % 2, :], copy).then_inc(wq_rounded, 1)
            walk(act, stage)

        @block.vector
        def _(dve):
            dve.memset(row_buf[:, :], 0.0).then_inc(zeroed, 1)
            for t, value in ((mask[:, :], 0.0), (ident[:, :], 0.0), (ones[:, :].bitcast(F32), 1.0)):
                dve.memset(t, value).then_inc(zeroed, 1)
            dve.memset(pt3_hi[:, :, :].bitcast(F32), 0.0).then_inc(zeroed, 1)
            dve.memset(pt3_lo[:, :, :].bitcast(F32), 0.0).then_inc(pv_free, 1)

            dve.wait_ge(const_in, 128)
            dve.wait_ge(edge_in, 144)
            steps = [0]

            def step(ins):
                ins.then_inc(edge_step, 1)
                steps[0] += 1
                dve.wait_ge(edge_step, steps[0])
            rows = row_buf[0:96, :]
            step(dve.tensor_scalar(rows, rows, edge_consts[:, 2:3], None, ALU.mult))
            step(dve.tensor_copy(edges[:, :], rows))
            step(dve.tensor_tensor(rows, rows, edges[:, :], ALU.subtract))
            step(dve.tensor_copy(edges[32:64, :], row_buf[32:64, :]))
            step(dve.tensor_copy(edges[64:96, :], row_buf[64:96, :]))
            step(dve.tensor_tensor(row_buf[64:96, :], row_buf[64:96, :], edges[64:96, :], ALU.subtract))
            step(dve.tensor_copy(edges[64:96, :], row_buf[64:96, :]))
            step(dve.tensor_scalar(coef_all[:, :], h_tok[0:96, 0:2, :].rearrange("p a n -> p (a n)").bitcast(I32),
                                   edge_consts[:, 0:1], edge_consts[:, 1:2], ALU.mult, ALU.is_ge))
            step(dve.tensor_scalar(rows_all[:, :], xi[:, :], 0, VOCAB - 1, ALU.max, ALU.min))
            step(dve.tensor_scalar(perm_now[:, :], perm[:, :], -E, None, ALU.add))
            dve.wait_ge(selected, 2)

            def centre(b, i):
                if i >= 2:
                    dve.wait_ge(squared, 8 * b + (i - 1))
                dve.tensor_tensor((rstd2 if i % 2 else y_raw)[:, :], hacc[:, i, :], mean2[:, :], ALU.subtract)\
                   .then_inc(y_step, 1)

            def stage(place):
                b, n = place.b, place.n
                N = 4 * n
                nb = 0 if place.kind == "start" else b + 1
                for s in place.steps:
                    i = int(s[-1]) if s[-1].isdigit() else 0
                    if s[0] == "S" and s != "ST":
                        for t in range(TT):
                            bank, c = SC_AT[t]
                            w = P * (t + 1)
                            if t != 1:
                                dve.wait_ge(sc_full, 3 * N + (3 * i + max(t, 1)))
                                dve.sem_inc(apart, 1)
                            at = sc[:, bank, c:c + w]
                            dve.tensor_tensor_reduce(at, at, mask[:, S - w:S], 1.0, LOWEST, ALU.add, ALU.max,
                                                     row_max[:, t:t + 1]).then_inc(tile_max, 1)
                        dve.wait_ge(tile_max, 4 * N + (4 * i + 4))
                        dve.tensor_scalar(neg_max[:, :], row_max[:, :], -SCALE, None, ALU.mult).then_inc(max_ready, 1)
                    elif s[0] == "N":
                        dve.wait_ge(exp_done, 4 * N + (4 * i + 4))
                        dve.reciprocal(inv_sum[:, :], row_sum[:, :]).then_inc(inv_ready, 1)
                        dve.wait_ge(inv_ready, N + (i + 1))
                        for t in range(TT):
                            at = prob[:, P_OFF[t]:P_OFF[t] + P * (t + 1)]
                            dve.tensor_scalar(at, at, inv_sum[:, t:t + 1], None, ALU.mult).then_inc(prob_ready, 1)
                    elif s[:2] == "Ta":
                        r = i % 2
                        base = 18 * n + 2
                        dve.wait_ge(tp_hi, base + (4 * i + 1))
                        dve.tensor_tensor(pt_lo[:, r, 0:S], tp[:, 0, :], pt_hi[:, r, 0:S], ALU.subtract)\
                           .then_inc(tpa_free, 1)
                        dve.wait_ge(tp_hi, base + (4 * i + 3))
                        dve.tensor_tensor(pt_lo[:, r, S:896], tp[:, 1, 0:384], pt_hi[:, r, S:896], ALU.subtract)
                        dve.tensor_tensor(pt3_lo[:, r, P:2 * P], tp[:, 1, 384:S], pt3_hi[:, r, P:2 * P],
                                          ALU.subtract).then_inc(tpb_free, 1)
                    elif s[:2] == "Tb":
                        r = i % 2
                        dve.wait_ge(tp_hi, 18 * n + (2 + 4 * i + 4))
                        dve.tensor_tensor(pt_lo[:, r, 896:PT_LEN], tp[:, 0, 0:256], pt_hi[:, r, 896:PT_LEN],
                                          ALU.subtract).then_inc(tpa_free, 1)
                    elif s[:2] == "PV":
                        dve.wait_ge(at_rounded, N + (i + 1))
                        dve.tensor_tensor(at_lo[:, i, :], pv[:, :], at_hi[:, i, :], ALU.subtract).then_inc(pv_free, 1)
                    elif s[0] in "QK":
                        hi, lo = (k_hi[:, :], k_lo[:, :]) if s == "K" else (q_hi[:, i % 2, :], q_lo[:, i % 2, :])
                        dve.wait_ge(split_hi, place.split_done(s))
                        dve.tensor_tensor(lo, fb[:, place.bank(s), :], hi, ALU.subtract)\
                           .then_inc(bank_free[place.bank(s)], 1)
                    elif s == "VT":
                        base = 0 if place.kind == "start" else (18 * n + 18 if place.kind != "post" else 18 * (8 * b + 8))
                        for half, free in ((0, tpa_free), (1, tpb_free)):
                            dve.wait_ge(tp_hi, base + (half + 1))
                            dve.tensor_tensor(v_lo[:, 2 * half:2 * half + 2, :],
                                              tp[:, half, 0:256].rearrange("p (j d) -> p j d", j=2),
                                              v_hi[:, 2 * half:2 * half + 2, :], ALU.subtract).then_inc(free, 1)
                    elif s[0] == "D":
                        dve.wait_ge(job_full, place.full(s))
                        dve.tensor_tensor(hacc[:, i, :], hacc[:, i, :], fb[:, place.bank(s), :], ALU.add)\
                           .then_inc(bank_free[place.bank(s)], 1)
                    elif s == "H0":
                        dve.wait_ge(hacc_free, b + 1)
                        dve.tensor_scalar(perm_now[:, :], perm_now[:, :], E, None, ALU.add).then_inc(perm_ready, 1)
                    elif s == "G":
                        dve.tensor_copy(rows_now[:, :], rows_all[:, bass.ds(TT * nb, TT)]).then_inc(rows_ready, 1)
                        dve.tensor_copy(coef[:, :], coef_all[:, bass.ds(S * nb, S)]).then_inc(rows_ready, 1)
                    elif s[0] == "B":
                        c, half = i // 2, i % 2
                        at = h_tok[:, c, half * S:(half + 1) * S]
                        if half == 0:
                            dve.wait_ge(pos_added, 4 * nb + (c + 1))
                        dve.wait_ge(b_full, 8 * nb + (i + 1))
                        dve.tensor_tensor(at, at, sc[:, 1 + half, :], ALU.add).then_inc(b_free, 1)
                        dve.wait_ge(b_free, 8 * nb + (i + 2))
                        dve.bn_stats(stats[:, c, half, :], at).then_inc(h_step, 1)
                        if half == 1:
                            dve.wait_ge(h_step, 15 * nb + (3 * c + 2))
                            dve.sem_inc(apart, 1)
                            dve.bn_aggr(moments[:, c, :], stats[:, c, :, :]).then_inc(h_step, 1)
                    elif s == "La":
                        dve.wait_ge(h_step, 15 * nb + 12)
                        dve.tensor_scalar(var_eps[:, :], moments[:, :, 1], EPS, None, ALU.add).then_inc(h_step, 1)
                        dve.wait_ge(h_step, 15 * nb + 13)
                        dve.reciprocal(inv_var[:, :], var_eps[:, :]).then_inc(h_step, 1)
                    elif s == "Lb":
                        dve.wait_ge(rstd_done, nb + 1)
                        dve.scalar_tensor_tensor(out=shift[:, :], in0=moments[:, :, 0], scalar=-1.0, in1=rstd[:, :],
                                                 op0=ALU.mult, op1=ALU.mult).then_inc(h_step, 1)
                    elif s[0] == "X":
                        c, half = i // 2, i % 2
                        at = (slice(None), slice(4 * half, 4 * half + 4), slice(c * P, (c + 1) * P))
                        dve.wait_ge(x_hi, 8 * nb + (i + 1))
                        dve.tensor_tensor(xn_lo[at], tp[:, half, :].rearrange("p (j t) -> p j t", j=4),
                                          xn_hi[at], ALU.subtract).then_inc(x_free, 1)
                    elif s[0] == "M":
                        dve.wait_ge(y_rounded, 24 * b + (i + 1))
                        dve.tensor_tensor(y_lo[:, i % 2, :], hacc[:, i, :], y_hi[:, i % 2, :], ALU.subtract)\
                           .then_inc(y_ready, 1)
                        if i == KT - 1:
                            dve.wait_ge(stat_full, 16 * b + 8)
                            dve.tensor_scalar(mean2[:, :], sc[:, 1, :], 1.0 / E, None, ALU.mult).then_inc(y_step, 1)
                            dve.wait_ge(y_step, 27 * b + 1)
                            centre(b, 0)
                            centre(b, 1)
                    elif s[0] == "R":
                        dve.wait_ge(y_rounded, 24 * b + (8 + i + 1))
                        dve.tensor_tensor(y_lo[:, i % 2, :], g_raw[:, i % 2, :], y_hi[:, i % 2, :],
                                          ALU.subtract).then_inc(y_ready, 1)
                        if i + 2 < KT:
                            centre(b, i + 2)
                        if i == KT - 1:
                            dve.wait_ge(stat_full, 16 * b + 16)
                            dve.tensor_scalar(rstd2[:, :], sc[:, 2, :], 1.0 / E, EPS, ALU.mult, ALU.add)\
                               .then_inc(y_step, 1)
                            dve.wait_ge(y_step, 27 * b + 10)
                            dve.reciprocal(y_raw[:, :], rstd2[:, :]).then_inc(y_step, 1)
                    elif s == "F":
                        mlp(place)

            def mlp(place):
                b = place.b
                first_job = len(place.jobs)

                def normalise(p):
                    dve.wait_ge(turned[p], 16 * b + 16)
                    dve.tensor_tensor(y_raw[:, :], hacc[:, p, :], mean2[:, :], ALU.subtract).then_inc(y_step, 1)
                    dve.wait_ge(y_step, 27 * b + (12 + 2 * p))
                    dve.tensor_tensor(y_raw[:, :], y_raw[:, :], rstd2[:, :], ALU.mult).then_inc(y_step, 1)

                def input_lo(p):
                    dve.wait_ge(y_rounded, 24 * b + (16 + p + 1))
                    dve.tensor_tensor(y_lo[:, p % 2, :], y_raw[:, :], y_hi[:, p % 2, :], ALU.subtract)\
                       .then_inc(y_ready, 1)

                def add_output(p):
                    dve.wait_ge(pv_full, 40 * b + (33 + p))
                    dve.tensor_tensor(hacc[:, p, :], hacc[:, p, :], pv[:, :], ALU.add).then_inc(pv_free, 1)

                dve.wait_ge(rstd2_done, b + 1)
                normalise(0)
                input_lo(0)
                for u in range(UNITS):
                    p, w = u // 4, u % 4
                    job = first_job + u
                    dve.wait_ge(bank_free[job % 2], place.half + (job // 2 + 1))
                    dve.tensor_copy(g_hi[:, w // 2, w % 2, :], gelu_out(w)).then_inc(g_rounded, 1)
                    if w > 0:
                        dve.wait_ge(g_rounded, 32 * b + (u + 1))
                        dve.tensor_tensor(g_lo[:, w // 2, w % 2, :], gelu_out(w), g_hi[:, w // 2, w % 2, :],
                                          ALU.subtract).then_inc(g_low_dve, 1)
                    if w == 0 and p + 1 < PAIRS:
                        normalise(p + 1)
                    if w == 2 and p + 1 < PAIRS:
                        input_lo(p + 1)
                    if w == 3 and p > 0:
                        add_output(p - 1)
                add_output(PAIRS - 1)

            walk(dve, stage)

        @block.gpsimd
        def _(pool):
            pool.sem_inc(wd_ready, 2)
            pool.sem_inc(up_ready, 1)
            pool.sem_inc(dn_ready, 1)
            pool.sem_inc(b_free, 1)
            pool.sem_inc(hacc_free, 1)
            pool.wait_ge(zeroed, 3)
            pool.affine_select(out=mask[:, S - P:S], in_=mask[:, S - P:S], compare_op=ALU.is_ge, fill=LOWEST,
                               base=0, pattern=[[-1, P]], channel_multiplier=1).then_inc(selected, 1)
            pool.affine_select(out=ident[:, :], in_=ident[:, :], compare_op=ALU.not_equal, fill=1.0,
                               base=0, pattern=[[-1, P]], channel_multiplier=1).then_inc(selected, 1)

            def low_wq(place, k):
                first = {"start": 0, "post": 48}.get(place.kind, 4)
                raw, slot = (first + k) % 2, (first + k) % RQ
                pool.wait_ge(wq_rounded, place.wq + (k + 1))
                pool.tensor_tensor(wq_lo[:, slot, :], wq_raw[:, raw, :], wq_hi[:, slot, :], ALU.subtract)\
                    .then_inc(wq_ready, 1)

            def low_wd(count, m):
                pool.wait_ge(wd_rounded, count + (m + 1))
                pool.tensor_tensor(wd_lo[:, m % RD, :], wd_raw[:, m % 2, :], wd_hi[:, m % RD, :], ALU.subtract)\
                    .then_inc(wd_ready, 1)

            def low_up(b, p):
                pool.wait_ge(up_rounded, 8 * b + (p + 1))
                pool.tensor_tensor(up_lo[:, p % 2, :], up_raw[:, :], up_hi[:, p % 2, :], ALU.subtract)\
                    .then_inc(up_ready, 1)

            def low_down(b, p):
                pool.wait_ge(dn_rounded, 8 * b + (p + 1))
                pool.tensor_tensor(dn_lo[:, p % 2, :], dn_raw[:, :], dn_hi[:, p % 2, :], ALU.subtract)\
                    .then_inc(dn_ready, 1)

            def stage(place):
                b = place.b
                nb = 0 if place.kind == "start" else b + 1
                if place.kind == "first":
                    for m in range(RD):
                        low_wd(64 * b, m)
                for s in place.steps:
                    i = int(s[-1]) if s[-1].isdigit() else 0
                    if is_qkv(s) and not (place.kind == "last" and "B0" not in place.steps):
                        low_wq(place, place.weights[s] + RQ)
                    if s[0] == "D" and not (place.kind == "post" and i >= RD):
                        low_wd(place.wd, i + RD)
                    if s == "G":
                        pool.wait_ge(rows_ready, 2 * nb + 1)
                        if place.kind == "start":
                            pool.wait_ge(edge_step, 8)
                        else:
                            pool.wait_ge(job_full, place.full("H7"))
                            pool.sem_inc(apart, 1)
                        for c in range(TT):
                            pool.indirect_dma_start(
                                out=h_tok[:, c, :], out_offset=None, in_=table,
                                in_offset=bass.IndirectOffsetOnAxis(ap=rows_now[:, c:c + 1].bitcast(U32), axis=0))\
                                .then_inc(gathered, 16)
                    if s[0] == "A":
                        if i == 0:
                            pool.wait_ge(gathered, 64 * nb + 64)
                        pool.wait_ge(pos_in, 64 * nb + 16 * (i + 1))
                        pool.tensor_tensor(h_tok[:, i, :], h_tok[:, i, :], row_buf[:, :], ALU.add)\
                            .then_inc(pos_added, 1)
                    if s[0] == "R":
                        if i == 0:
                            pool.wait_ge(stored, 128 * b + 128)
                        pool.wait_ge(y_step, 27 * b + (i + 2))
                        pool.sem_inc(apart, 1)
                        pool.indirect_dma_start(
                            out=hacc[:, i, :], out_offset=None, in_=scratch,
                            in_offset=bass.IndirectOffsetOnAxis(ap=perm[:, i:i + 1].bitcast(U32), axis=0))\
                            .then_inc(turned[i], 16)
                    if s == "F":
                        mlp(b)

            def mlp(b):
                def scatter(p):
                    pool.wait_ge(pv_free, 40 * b + (34 + p))
                    pool.sem_inc(apart, 1)
                    pool.indirect_dma_start(
                        out=out, out_offset=bass.IndirectOffsetOnAxis(ap=perm_now[:, p:p + 1].bitcast(U32), axis=0),
                        in_=hacc[:, p, :], in_offset=None).then_inc(scattered, 16)

                low_up(b, 0)
                low_down(b, 0)
                pool.wait_ge(perm_ready, b + 1)
                for u in range(UNITS):
                    p, w = u // 4, u % 4
                    if w == 0:
                        pool.wait_ge(g_rounded, 32 * b + (u + 1))
                        pool.tensor_tensor(g_lo[:, 0, 0, :], gelu_out(0), g_hi[:, 0, 0, :], ALU.subtract)\
                            .then_inc(g_low_pool, 1)
                        if p + 1 < PAIRS:
                            low_up(b, p + 1)
                    if w == 3 and p > 0:
                        scatter(p - 1)
                    if w == 3 and p + 1 < PAIRS:
                        low_down(b, p + 1)
                scatter(PAIRS - 1)
                pool.wait_ge(scattered, 128 * b + 128)
                pool.sem_inc(hacc_free, 1)

            start = Place([], 0, 0, "start")
            for m in range(RQ):
                low_wq(start, m)
            walk(pool, stage)


def kernel(x, L0_tok_kernel, L0_tok_bias, L0_tok_pos_emb, L0_attn_w_qkv, L0_attn_w_dense,
           L0_ffn_up, L0_ffn_down, L0_ffn_perm):
    import numpy as np
    import concourse.bacc as bacc
    from concourse.bass_utils import run_bass_kernel_spmd

    x = np.asarray(x)
    x_cols = x.reshape(B * TT, P).T
    x_row = x.reshape(1, B * S)
    table = np.asarray(L0_tok_kernel).reshape(VOCAB, E)

    edge_cols = np.zeros((32, 3), np.float32)
    edge_cols[:, 1], edge_cols[:, 2] = 1, 1
    n = SHARDS - 1
    for s in range(n):
        edge_cols[s, 0:2] = 1, (s + 1) * VS
        edge_cols[n + s, 0:2] = -1, 1 - (s + 1) * VS
    edge_cols[2 * n] = 0, 0, SHARDS

    w = np.asarray(L0_attn_w_qkv).reshape(G * (HQ + 2), D, KT, P).transpose(0, 3, 2, 1).reshape(-1, P, E)
    order = []
    for g in range(G):
        q, k, v = g * HQ, G * HQ + g, G * HQ + G + g
        order += [q, k, q + 1, v, q + 2, q + 3]
    w_qkv = w[order + order[:RQ]]
    w_dense = np.asarray(L0_attn_w_dense).reshape(KT, P, G, HQ, D).transpose(2, 0, 4, 3, 1)\
        .reshape(G * KT, P, HQ * P)
    w_up = np.zeros((PAIRS, 2, DH, 2, MH), np.float32)
    w_down = np.zeros((PAIRS, P, 2, 2, 2, DH), np.float32)
    up = np.asarray(L0_ffn_up).reshape(PAIRS, 2, DH, MH)
    down = np.asarray(L0_ffn_down).reshape(PAIRS, 2, 2, P, DH)
    for h in range(2):
        w_up[:, h, :, h, :] = up[:, h]
        w_down[:, :, h, :, h, :] = down[:, h].transpose(0, 2, 1, 3)
    w_up, w_down = w_up.reshape(PAIRS, P, 2 * MH), w_down.reshape(PAIRS, P, 4 * P)
    perm_cols = np.asarray(L0_ffn_perm).reshape(KT, P).T

    arrays = {
        "x_cols": x_cols, "x_row": x_row, "table": table,
        "bias": np.asarray(L0_tok_bias).reshape(1, E), "pos": np.asarray(L0_tok_pos_emb),
        "edge_cols": edge_cols, "w_qkv": w_qkv, "w_dense": w_dense, "w_up": w_up, "w_down": w_down, "perm_cols": perm_cols,
    }
    arrays = {name: np.ascontiguousarray(a) for name, a in arrays.items()}
    nc = bacc.Bacc("TRN2", target_bir_lowering=False, num_devices=1)
    args = [nc.dram_tensor(f"in_{name}", a.shape, mybir.dt.from_np(a.dtype), kind="ExternalInput").ap()
            for name, a in arrays.items()]
    out = nc.dram_tensor("out_rows", [B * E, S], F32, kind="ExternalOutput").ap()
    tower_kernel(nc, *args, out)
    r = run_bass_kernel_spmd(nc, [{f"in_{name}": a for name, a in arrays.items()}], core_ids=[0])
    rows = r.results[0]["out_rows"]
    return rows.reshape(B, E, S).transpose(0, 2, 1)
```
